# Optimizing a Trainium2 kernel written in Bass

```python
import numpy as np
import jax
import jax.numpy as jnp

def _softmax(x, axis=-1):
    return jax.nn.softmax(x, axis=axis)
def _gelu(x):
    return jax.nn.gelu(x, approximate=True)
def _silu(x):
    return jax.nn.silu(x)
def _sigmoid(x):
    return jax.nn.sigmoid(x)
def _layernorm(x, axis=-1, eps=1e-5):
    m = jnp.mean(x, axis=axis, keepdims=True)
    v = jnp.var(x, axis=axis, keepdims=True)
    return (x - m) / jnp.sqrt(v + eps)
def _scatter_add(tgt, idx, src, axis=0):
    return tgt.at[idx].add(src)
def _segment_sum(src, seg, n):
    return jax.ops.segment_sum(src, seg, n)

kernel_name = 'mk_conv_preact_d1_conv_nchw512_bfe97b'

def setup_inputs(seed: int = 0):
    np.random.seed(seed)
    _w = jnp.asarray
    def _rec_inputs():
        import jax
        import jax.numpy as jnp
        _gk = jax.random.key(seed)
        x = -7.109e-05 + 0.9999 * jax.random.normal(jax.random.fold_in(_gk, 1), (32, 512, 64, 64), jnp.float32)
        return x
    x = _rec_inputs()
    def _L0_conv_setup():
        import jax, jax.numpy as jnp
        from jax import lax
        import numpy as np
        EPS = 1e-05
        HEADS, DIM_K, R = (4, 16, 15)
        PAD = (R - 1) // 2

        def bn(x, g, b, m, v):
            scale = g * lax.rsqrt(v + EPS)
            return x * scale[None, :, None, None] + (b - m * scale)[None, :, None, None]

        def conv1x1(x, w):
            return jnp.einsum('bchw,oc->bohw', x, w)

        def position_lambdas(emb, values):
            B, V, H, W = values.shape
            vals = values.reshape(B * V, 1, H, W)
            out = lax.conv_general_dilated(vals, emb[:, None, :, :], (1, 1), [(PAD, PAD), (PAD, PAD)])
            out = out.reshape(B, V, DIM_K, H, W).transpose(0, 2, 1, 3, 4)
            return out.reshape(B, DIM_K, V, H * W)

        def lambda_layer(x, q_w, bnq_g, bnq_b, bnq_m, bnq_v, k_w, v_w, bnv_g, bnv_b, bnv_m, bnv_v, emb):
            B, _, H, W = x.shape
            q = bn(conv1x1(x, q_w), bnq_g, bnq_b, bnq_m, bnq_v)
            k = conv1x1(x, k_w)
            v = bn(conv1x1(x, v_w), bnv_g, bnv_b, bnv_m, bnv_v)
            pos = position_lambdas(emb, v)
            k = jax.nn.softmax(k, axis=1)
            dim_v = v.shape[1]
            q = q.reshape(B, HEADS, DIM_K, H * W)
            k = k.reshape(B, DIM_K, H * W)
            v2 = v.reshape(B, dim_v, H * W)
            content_lambda = jnp.einsum('bkm,bvm->bkv', k, v2)
            content_out = jnp.einsum('bhkn,bkv->bhvn', q, content_lambda)
            position_out = jnp.einsum('bhkn,bkvn->bhvn', q, pos)
            out = content_out + position_out
            return out.reshape(B, HEADS * dim_v, H, W)
        key = jax.random.key(seed)
        ks = jax.random.split(key, 32)
        inplanes, width, outplanes = (512, 128, 512)
        dim_v = width // HEADS
        B, H, W = (32, 64, 64)
        n = lambda i, shape, s=1.0: jax.random.normal(ks[i], shape, jnp.float32) * s
        u = lambda i, shape: jax.random.uniform(ks[i], shape, jnp.float32, 0.5, 1.5)
        return {'x': n(0, (B, inplanes, H, W)), 'conv1_w': n(1, (width, inplanes), 0.05), 'bn1_g': u(2, (width,)), 'bn1_b': n(3, (width,), 0.1), 'bn1_m': n(4, (width,), 0.1), 'bn1_v': u(5, (width,)), 'q_w': n(6, (DIM_K * HEADS, width), 0.05), 'bnq_g': u(7, (DIM_K * HEADS,)), 'bnq_b': n(8, (DIM_K * HEADS,), 0.1), 'bnq_m': n(9, (DIM_K * HEADS,), 0.1), 'bnq_v': u(10, (DIM_K * HEADS,)), 'k_w': n(11, (DIM_K, width), 0.05), 'v_w': n(12, (dim_v, width), 0.05), 'bnv_g': u(13, (dim_v,)), 'bnv_b': n(14, (dim_v,), 0.1), 'bnv_m': n(15, (dim_v,), 0.1), 'bnv_v': u(16, (dim_v,)), 'emb': n(17, (DIM_K, R, R), 0.1), 'bn2_g': u(18, (width,)), 'bn2_b': n(19, (width,), 0.1), 'bn2_m': n(20, (width,), 0.1), 'bn2_v': u(21, (width,)), 'conv3_w': n(22, (outplanes, width), 0.05), 'bn3_g': u(23, (outplanes,)), 'bn3_b': n(24, (outplanes,), 0.1), 'bn3_m': n(25, (outplanes,), 0.1), 'bn3_v': u(26, (outplanes,))}
    _L0_conv_all = _L0_conv_setup()
    _L0_conv_in = {k: v for k, v in _L0_conv_all.items() if k in ('conv1_w', 'bn1_g', 'bn1_b', 'bn1_m', 'bn1_v', 'q_w', 'bnq_g', 'bnq_b', 'bnq_m', 'bnq_v', 'k_w', 'v_w', 'bnv_g', 'bnv_b', 'bnv_m', 'bnv_v', 'emb', 'bn2_g', 'bn2_b', 'bn2_m', 'bn2_v', 'conv3_w', 'bn3_g', 'bn3_b', 'bn3_m', 'bn3_v', )}
    del _L0_conv_all

    return {
        "x": x,
        "L0_conv_conv1_w": _L0_conv_in["conv1_w"],
        "L0_conv_bn1_g": _L0_conv_in["bn1_g"],
        "L0_conv_bn1_b": _L0_conv_in["bn1_b"],
        "L0_conv_bn1_m": _L0_conv_in["bn1_m"],
        "L0_conv_bn1_v": _L0_conv_in["bn1_v"],
        "L0_conv_q_w": _L0_conv_in["q_w"],
        "L0_conv_bnq_g": _L0_conv_in["bnq_g"],
        "L0_conv_bnq_b": _L0_conv_in["bnq_b"],
        "L0_conv_bnq_m": _L0_conv_in["bnq_m"],
        "L0_conv_bnq_v": _L0_conv_in["bnq_v"],
        "L0_conv_k_w": _L0_conv_in["k_w"],
        "L0_conv_v_w": _L0_conv_in["v_w"],
        "L0_conv_bnv_g": _L0_conv_in["bnv_g"],
        "L0_conv_bnv_b": _L0_conv_in["bnv_b"],
        "L0_conv_bnv_m": _L0_conv_in["bnv_m"],
        "L0_conv_bnv_v": _L0_conv_in["bnv_v"],
        "L0_conv_emb": _L0_conv_in["emb"],
        "L0_conv_bn2_g": _L0_conv_in["bn2_g"],
        "L0_conv_bn2_b": _L0_conv_in["bn2_b"],
        "L0_conv_bn2_m": _L0_conv_in["bn2_m"],
        "L0_conv_bn2_v": _L0_conv_in["bn2_v"],
        "L0_conv_conv3_w": _L0_conv_in["conv3_w"],
        "L0_conv_bn3_g": _L0_conv_in["bn3_g"],
        "L0_conv_bn3_b": _L0_conv_in["bn3_b"],
        "L0_conv_bn3_m": _L0_conv_in["bn3_m"],
        "L0_conv_bn3_v": _L0_conv_in["bn3_v"],
    }

def reference(x, L0_conv_conv1_w, L0_conv_bn1_g, L0_conv_bn1_b, L0_conv_bn1_m, L0_conv_bn1_v, L0_conv_q_w, L0_conv_bnq_g, L0_conv_bnq_b, L0_conv_bnq_m, L0_conv_bnq_v, L0_conv_k_w, L0_conv_v_w, L0_conv_bnv_g, L0_conv_bnv_b, L0_conv_bnv_m, L0_conv_bnv_v, L0_conv_emb, L0_conv_bn2_g, L0_conv_bn2_b, L0_conv_bn2_m, L0_conv_bn2_v, L0_conv_conv3_w, L0_conv_bn3_g, L0_conv_bn3_b, L0_conv_bn3_m, L0_conv_bn3_v):
    import jax
    import jax.numpy as jnp
    def _L0_conv_ref(x, conv1_w, bn1_g, bn1_b, bn1_m, bn1_v, q_w, bnq_g, bnq_b, bnq_m, bnq_v, k_w, v_w, bnv_g, bnv_b, bnv_m, bnv_v, emb, bn2_g, bn2_b, bn2_m, bn2_v, conv3_w, bn3_g, bn3_b, bn3_m, bn3_v):
        import jax, jax.numpy as jnp
        from jax import lax
        import numpy as np
        EPS = 1e-05
        HEADS, DIM_K, R = (4, 16, 15)
        PAD = (R - 1) // 2

        def bn(x, g, b, m, v):
            scale = g * lax.rsqrt(v + EPS)
            return x * scale[None, :, None, None] + (b - m * scale)[None, :, None, None]

        def conv1x1(x, w):
            return jnp.einsum('bchw,oc->bohw', x, w)

        def position_lambdas(emb, values):
            B, V, H, W = values.shape
            vals = values.reshape(B * V, 1, H, W)
            out = lax.conv_general_dilated(vals, emb[:, None, :, :], (1, 1), [(PAD, PAD), (PAD, PAD)])
            out = out.reshape(B, V, DIM_K, H, W).transpose(0, 2, 1, 3, 4)
            return out.reshape(B, DIM_K, V, H * W)

        def lambda_layer(x, q_w, bnq_g, bnq_b, bnq_m, bnq_v, k_w, v_w, bnv_g, bnv_b, bnv_m, bnv_v, emb):
            B, _, H, W = x.shape
            q = bn(conv1x1(x, q_w), bnq_g, bnq_b, bnq_m, bnq_v)
            k = conv1x1(x, k_w)
            v = bn(conv1x1(x, v_w), bnv_g, bnv_b, bnv_m, bnv_v)
            pos = position_lambdas(emb, v)
            k = jax.nn.softmax(k, axis=1)
            dim_v = v.shape[1]
            q = q.reshape(B, HEADS, DIM_K, H * W)
            k = k.reshape(B, DIM_K, H * W)
            v2 = v.reshape(B, dim_v, H * W)
            content_lambda = jnp.einsum('bkm,bvm->bkv', k, v2)
            content_out = jnp.einsum('bhkn,bkv->bhvn', q, content_lambda)
            position_out = jnp.einsum('bhkn,bkvn->bhvn', q, pos)
            out = content_out + position_out
            return out.reshape(B, HEADS * dim_v, H, W)
        residual = x
        h = jax.nn.relu(bn(conv1x1(x, conv1_w), bn1_g, bn1_b, bn1_m, bn1_v))
        h = lambda_layer(h, q_w, bnq_g, bnq_b, bnq_m, bnq_v, k_w, v_w, bnv_g, bnv_b, bnv_m, bnv_v, emb)
        h = jax.nn.relu(bn(h, bn2_g, bn2_b, bn2_m, bn2_v))
        h = bn(conv1x1(h, conv3_w), bn3_g, bn3_b, bn3_m, bn3_v)
        return jax.nn.relu(h + residual)

    def _gn(v, G=32, eps=1e-5):
        B_, C_, H_, W_ = v.shape
        g = v.reshape(B_, G, C_ // G, H_, W_)
        m = jnp.mean(g, axis=(2, 3, 4), keepdims=True)
        s = jnp.var(g, axis=(2, 3, 4), keepdims=True)
        return ((g - m) / jnp.sqrt(s + eps)).reshape(v.shape)

    def _ln_c(v, eps=1e-6):
        m = jnp.mean(v, axis=1, keepdims=True)
        s = jnp.var(v, axis=1, keepdims=True)
        return (v - m) / jnp.sqrt(s + eps)

    def _ln_t(v, eps=1e-5):
        m = jnp.mean(v, axis=-1, keepdims=True)
        s = jnp.var(v, axis=-1, keepdims=True)
        return (v - m) / jnp.sqrt(s + eps)

    def _to_tokens(v):
        B_, C_, H_, W_ = v.shape
        return v.reshape(B_, C_, H_ * W_).transpose(0, 2, 1)
    def _from_tokens(t, like):
        B_, C_, H_, W_ = like.shape
        return t.transpose(0, 2, 1).reshape(B_, C_, H_, W_)

    x = x + _L0_conv_ref(_gn(x), L0_conv_conv1_w, L0_conv_bn1_g, L0_conv_bn1_b, L0_conv_bn1_m, L0_conv_bn1_v, L0_conv_q_w, L0_conv_bnq_g, L0_conv_bnq_b, L0_conv_bnq_m, L0_conv_bnq_v, L0_conv_k_w, L0_conv_v_w, L0_conv_bnv_g, L0_conv_bnv_b, L0_conv_bnv_m, L0_conv_bnv_v, L0_conv_emb, L0_conv_bn2_g, L0_conv_bn2_b, L0_conv_bn2_m, L0_conv_bn2_v, L0_conv_conv3_w, L0_conv_bn3_g, L0_conv_bn3_b, L0_conv_bn3_m, L0_conv_bn3_v)
    return x


_drawn_inputs = setup_inputs


def setup_inputs(seed=0):
    import zlib

    import numpy as np

    out = dict(_drawn_inputs(seed))
    spreads = {}
    factors = {'L0_conv_emb': 5.755,
     'L0_conv_bn2_b': 64.0,
     'L0_conv_bn2_m': 64.0,
     'L0_conv_bn3_b': 56.16,
     'L0_conv_bn3_m': 50.27}
    for name, (base, spread) in spreads.items():
        noise = np.random.default_rng([zlib.crc32(name.encode()), seed]).standard_normal(out[name].shape)
        drawn = base * np.exp(spread * noise) if base else spread * noise
        out[name] = jnp.asarray(drawn.astype(out[name].dtype))
    for name, factor in factors.items():
        out[name] = (out[name] * factor).astype(out[name].dtype)
    return out
```

```python
from contextlib import ExitStack

import concourse.bass as bass
from concourse import mybir

F32 = mybir.dt.float32
BF16 = mybir.dt.bfloat16
ALU = mybir.AluOpType
ACT = mybir.ActivationFunctionType
AX_X = mybir.AxisListType.X

P = 128
EPS = 1e-5
GROUPS = 32
R = 15
PAD = (R - 1) // 2
BY, BX = 4, 8
PIX = BY * BX
WX = BX + R - 1
TD = 5
NT = 4
KWIN = TD * WX
LASTD = BY + R - 1 - (NT - 1) * TD
NPART = 3
SPLIT = [(0, 0), (1, 0), (2, 0), (0, 1), (1, 1), (0, 2)]
CHUNK = 1024
STAT_STEPS = [2, 4, 5, 6, 8, 9, 10, 12]
GN_AFTER = {13: "gmean", 14: "gvar", 15: "bias1"}
VECTOR_YO = 1
WGEN_AT = [0, 6, 12, 18]


def front_order():
    return ["c0", "c1", "q0", "k0", "c2", "q1", "k1", "c3", "q2", "k2", "q3", "k3"]


def lambda_order(with_stats):
    order = ["cl"] + [f"w0.{yo}" for yo in range(BY)]
    for i in range(16):
        if i < 15:
            order += [f"w{i + 1}.{yo}" for yo in range(BY)]
        if with_stats and i in GN_AFTER:
            order.append(GN_AFTER[i])
    return order


def lambda_block(nc, x, w1, bn1, wq, bnq, wk, wv, bnv, emb, bn2, w3, bn3, out):
    B, C, H, W = x.shape
    N = H * W
    CT = C // P
    MID = w1.shape[0]
    QC = wq.shape[0]
    DK = wk.shape[0]
    DV = wv.shape[0]
    HEADS = QC // DK
    KV = DV + DK
    NCH = N // CHUNK
    HALF = 512
    NBY, NXB = H // BY, W // BX
    XQ = 2
    NQ = NXB // XQ
    NBLK = NBY * XQ
    UNITS = NQ * NT
    assert MID == P and HEADS * DV == P and HEADS * PIX == P and NCH == 4 and CT == 4 and NQ == 4
    VROWS = (NBY - 1) * BY + (NT - 1) * TD + 1
    XROWS = VROWS + TD - 1
    PT = N // P
    CPG = C // GROUPS
    KC = KWIN + DK
    EROWS = NT * TD + BY
    EOFF = BY * WX
    SLOTS = 4

    xv = x.rearrange("b (c p) h w -> b p c (h w)", p=P)
    ov = out.rearrange("b (c p) h w -> b p c (h w)", p=P)

    ctx = ExitStack()
    with ctx:
        def sb(name, shape, dt=F32):
            return ctx.enter_context(nc.sbuf_tensor(name, shape, dt))

        def sem(name):
            return ctx.enter_context(nc.semaphore(name))

        X = sb("X", [P, NCH, CT, CHUNK])
        region = sb("region", [P, 2 * NBLK * P])
        Q = sb("Q", [len(SPLIT) * DK, HEADS, N], BF16)
        h2 = sb("h2", [P, N])
        V = sb("V", [P, SLOTS, VROWS * DV])
        vX = sb("vX", [P, XROWS, DV])
        vS = sb("vS", [P, PT, DV])
        kS = sb("kS", [P, PT, DK])
        T = sb("T", [P, CHUNK])
        w1T = sb("w1T", [P, CT, MID])
        w1e = sb("w1e", [P, CT, MID])
        w3T = sb("w3T", [P, CT, P])
        wqT = sb("wqT", [P, QC])
        wkvT = sb("wkvT", [P, KV])
        grp = sb("grp", [P, P])
        ident = sb("ident", [P, P])
        Epad = sb("Epad", [len(SPLIT) * DK, EROWS * WX], BF16)
        Elast = sb("Elast", [len(SPLIT) * DK, PIX, KC], BF16)
        vbias = sb("vbias", [P, DV])
        st = sb("st", [P, CT, 2 * NCH, 6])
        mv = sb("mv", [P, CT, 2])
        par = sb("par", [P, 4, 8])
        psc = sb("psc", [P, 8])
        pbi = sb("pbi", [P, 8])
        g8 = sb("g8", [P, 4, 8])
        gmean = sb("gmean", [P, CT])
        gtmp = sb("gtmp", [P, CT])
        gve = sb("gve", [P, CT])
        gvar = sb("gvar", [P, CT])
        gsq = sb("gsq", [P, CT])
        rstd = sb("rstd", [P, CT])
        bnew = sb("bnew", [P, CT])
        rcur = sb("rcur", [P, CT])
        bcur = sb("bcur", [P, CT])
        nb1 = sb("nb1", [P, 1])
        kst = sb("kst", [P, PT])
        clS = sb("clS", [DK, DV])

        Wt = region[:, :].rearrange("p (u b n) -> p u b n", u=2, n=P)
        h1 = region[:, 0:2 * CHUNK].rearrange("p (u n) -> p u n", u=2)
        qp = region[0:QC, 2 * CHUNK:2 * CHUNK + NPART * N // 2].bitcast(BF16).rearrange(
            "p (a n) -> p a n", a=NPART)
        r1 = T[0:QC, :]
        Qv = Q[:, :, :].rearrange("p h (yb yo x) -> p h yb yo x", yo=BY, x=W)
        h2v = h2[:, :].rearrange("p (y x) -> p y x", x=W)
        Vv = V[:, :, :].rearrange("p s (y v) -> p s y v", v=DV)
        o = 0
        w1r = region[:, o:o + C]; o += C
        w3r = region[:, o:o + CT * P].rearrange("p (t n) -> p t n", t=CT); o += CT * P
        wqr = region[0:QC, o:o + MID]; o += MID
        wkvr = region[0:KV, o:o + MID]; o += MID
        vbb = region[0:DV, o:o + P]; o += P
        NE = len(SPLIT) * DK
        RR = R * R
        emb6 = region[0:NE, o:o + RR]; o += RR
        eres = region[0:NE, o:o + RR]; o += RR
        epart = [region[0:NE, o + 128 * a:o + 128 * a + 128].bitcast(BF16)[:, 0:RR] for a in range(NPART)]
        o += NPART * 128
        dlt = region[0:NE, o:o + DK]; o += DK
        Esel = region[0:NE, o:o + 128].bitcast(BF16)[:, 0:RR]; o += 128

        ring = [ctx.enter_context(nc.psum_tensor(f"ring{i}", [P, CHUNK], F32)) for i in range(3)]
        acc = [ctx.enter_context(nc.psum_tensor(f"acc{i}", [P, HALF], F32)) for i in range(2)]

        setup_in = sem("setup_in")
        setup_dve = sem("setup_dve")
        setup_pool = sem("setup_pool")
        setup_act = sem("setup_act")
        setup_gp = sem("setup_gp")
        setup_scaled = sem("setup_scaled")
        setup_pe = sem("setup_pe")
        setup_edma = sem("setup_edma")
        setup_parts = sem("setup_parts")
        ring_full = [sem(f"ring_full{i}") for i in range(3)]
        x_in = [sem(f"x_in{j}") for j in range(NCH)]
        res_in = [sem(f"res_in{j}") for j in range(NCH)]
        out_done = [sem(f"out_done{j}") for j in range(NCH)]
        stats_ready = sem("stats_ready")
        gmean_ready = sem("gmean_ready")
        sum_ready = sem("sum_ready")
        gvar_ready = sem("gvar_ready")
        sqrt_done = sem("sqrt_done")
        w1e_ready = sem("w1e_ready")
        nb1_ready = sem("nb1_ready")
        h1_ready = sem("h1_ready")
        qh_ready = sem("qh_ready")
        r1_ready = sem("r1_ready")
        qm_done = sem("qm_done")
        qparts_ready = sem("qparts_ready")
        q_in = sem("q_in")
        vs_ready = sem("vs_ready")
        vx_ready = sem("vx_ready")
        kmax_done = sem("kmax_done")
        kexp_done = sem("kexp_done")
        soft_ready = sem("soft_ready")
        cl_ready = sem("cl_ready")
        content_in = sem("content_in")
        v_in = [sem(f"v_in{s}") for s in range(SLOTS)]
        w_by_act = sem("w_by_act")
        w_by_dve = sem("w_by_dve")
        half_done = sem("half_done")
        t_ready = sem("t_ready")
        h2_ready = sem("h2_ready")
        out_ready = sem("out_ready")
        dve_link = sem("dve_link")

        HEAD = 1

        GN_USES = ["gmean", "gvar", "bias1"]
        FRONT = front_order()
        LAM = lambda_order(True)
        LAM_END = lambda_order(False)
        OUT = [f"o{j}.{t}" for j in range(NCH) for t in range(CT)]
        FIRST = len(GN_USES) + len(FRONT)
        PER = len(LAM) + len(FRONT) + len(OUT)
        assert PER % 3 == 0

        class Uses:
            def __init__(self, order, start, it):
                self.order, self.it = order, it
                self.at = {name: n for n, (name, _b) in enumerate(order)}
                self.start = start

            def slot(self, name):
                return (self.start + self.at[name]) % 3

            def full(self, name):
                return self.it * (PER // 3) + (self.start + self.at[name]) // 3 + 1

            def before(self, name):
                n = self.at[name] - 3
                return self.order[n] if n >= 0 else None

        def moved(name, b):
            if name == "cl":
                return cl_ready, b + 1
            if name in GN_USES:
                return {"gmean": gmean_ready, "gvar": gvar_ready, "bias1": nb1_ready}[name], b + 1
            kind = name[0]
            if kind == "w":
                i, yo = (int(a) for a in name[1:].split("."))
                if yo == VECTOR_YO:
                    return w_by_dve, b * UNITS + i + 1
                return w_by_act, b * ((BY - 1) * UNITS) + (BY - 1) * i + (yo if yo < VECTOR_YO else yo - 1) + 1
            if kind == "o":
                j, t = (int(a) for a in name[1:].split("."))
                return sum_ready, b * (NCH * CT) + HEAD + j * CT + t + 1
            return {"c": h1_ready, "q": r1_ready, "k": vs_ready}[kind], b * NCH + int(name[1]) + 1

        def images(order, b):
            return [(name, b) for name in order]

        def uses_before_loop():
            return Uses(images(GN_USES + FRONT, 0), 0, 0)

        def uses_in_loop(b):
            order = [(name, b + 1 if name in GN_USES else b) for name in LAM]
            return Uses(order + images(FRONT, b + 1) + images(OUT, b), FIRST, b)

        def uses_after_loop():
            return Uses(images(LAM_END + OUT, B - 1), FIRST, B - 1)

        block = ctx.enter_context(nc.Block())

        @block.sync
        def _(sp):
            def load_x(b, j):
                sp.dma_start(X[:, j, :, :], xv[b, :, :, j * CHUNK:(j + 1) * CHUNK]).then_inc(x_in[j], 16)

            def load_windows(xb):
                s = xb % SLOTS
                x0 = xb * BX - PAD
                left = max(0, -x0)
                for d in range(TD):
                    if left:
                        sp.dma_start(Vv[d * WX:d * WX + left, s, :, :],
                                     vX[W:W + left, d:d + VROWS, :]).then_inc(v_in[s], 16)
                    sp.dma_start(Vv[d * WX + left:(d + 1) * WX, s, :, :],
                                 vX[x0 + left:x0 + WX, d:d + VROWS, :]).then_inc(v_in[s], 16)

            def spread_q(b):
                sp.wait_ge(qparts_ready, b * NCH + NCH)
                for g, (a, _e) in enumerate(SPLIT):
                    for h in range(HEADS):
                        sp.dma_start(Q[g * DK:(g + 1) * DK, h, :],
                                     qp[h * DK:(h + 1) * DK, a, :]).then_inc(q_in, 16)

            def first_windows(b):
                sp.wait_ge(vx_ready, b * (2 * NCH) + 2 * NCH)
                for xb in range(SLOTS):
                    load_windows(xb)

            def during_lambda(b, last):
                sp.wait_ge(cl_ready, b + 1)
                for s in range(SLOTS):
                    sp.dma_start(Vv[KWIN:KC, s, (NT - 1) * TD:VROWS:BY, :],
                                 clS[:, :].unsqueeze(1).to_broadcast([DK, NBY, DV])).then_inc(content_in, 16)
                if not last:
                    for j in range(NCH):
                        sp.wait_ge(out_done[j], b * (16 * CT) + HEAD)
                        load_x(b + 1, j)
                for q in range(NQ - SLOTS // XQ):
                    sp.wait_ge(half_done, b * (2 * UNITS) + 2 * NT * (q + 1))
                    for xb in range(SLOTS + XQ * q, SLOTS + XQ * (q + 1)):
                        load_windows(xb)

            def during_output(b):
                for j in range(NCH):
                    for t in range(CT):
                        sp.wait_ge(out_ready, b * (NCH * CT) + j * CT + t + 1)
                        sp.dma_start(ov[b, :, t, j * CHUNK:(j + 1) * CHUNK],
                                     X[:, j, t, :]).then_inc(out_done[j], 16)

            def reload(b, j):
                sp.dma_start(X[:, j, :, :], xv[b, :, :, j * CHUNK:(j + 1) * CHUNK]).then_inc(res_in[j], 16)

            for j in range(NCH):
                sp.sem_inc(out_done[j], HEAD)
                load_x(0, j)
            sp.dma_start(w1r, w1).then_inc(setup_in, 16)
            sp.dma_start(w3r, w3.rearrange("(t p) c -> p t c", p=P)).then_inc(setup_in, 16)
            sp.dma_start(wqr, wq).then_inc(setup_in, 16)
            sp.dma_start(wkvr[0:DV, :], wv).then_inc(setup_in, 16)
            sp.dma_start(wkvr[DV:KV, :], wk).then_inc(setup_in, 16)
            for g in range(len(SPLIT)):
                sp.dma_start(emb6[g * DK:(g + 1) * DK, :], emb.rearrange("k a b -> k (a b)")).then_inc(setup_in, 16)
            sp.wait_ge(setup_pool, 1)
            for n, (bn, size) in enumerate([(bn1, MID), (bn2, P), (bnq, QC), (bnv, DV)]):
                for a in range(4):
                    sp.dma_start(par[0:size, a, n:n + 1],
                                 bn[a].rearrange("(p a) -> p a", a=1)).then_inc(setup_in, 16)
            for a in range(4):
                for t in range(CT):
                    sp.dma_start(par[:, a, 4 + t:5 + t],
                                 bn3[a][t * P:(t + 1) * P].rearrange("(p a) -> p a", a=1)).then_inc(setup_in, 16)
            sp.wait_ge(setup_parts, 3)
            for g, (_a, e) in enumerate(SPLIT):
                sp.dma_start(Esel[g * DK:(g + 1) * DK, :], epart[e][g * DK:(g + 1) * DK, :]).then_inc(setup_edma, 16)

            spread_q(0)
            first_windows(0)
            with sp.Fori(0, B - 1) as b:
                u = uses_in_loop(b)
                during_lambda(b, False)
                for j in range(NCH):
                    sp.wait_ge(ring_full[u.slot(f"c{j}")], u.full(f"c{j}"))
                    reload(b, j)
                spread_q(b + 1)
                first_windows(b + 1)
                during_output(b)
            e = B - 1
            during_lambda(e, True)
            for j in range(NCH):
                sp.wait_ge(out_done[j], e * (16 * CT) + HEAD)
                reload(e, j)
            during_output(e)
            for j in range(NCH):
                sp.wait_ge(out_done[j], B * 16 * CT + HEAD)

        N_SETUP_IN = 16 * (5 + len(SPLIT) + 16 + 4 * CT)

        @block.tensor
        def _(pe):
            def take(u, name):
                s = u.slot(name)
                prior = u.before(name)
                if prior:
                    pe.wait_ge(*moved(*prior))
                return ring[s], ring_full[s]

            def gn_product(u, b, name):
                if name == "gmean":
                    pe.wait_ge(stats_ready, b * 2 + 1)
                    dst, full = take(u, name)
                    nc.tensor.matmul(dst[:, 0:CT], grp[:, :], mv[:, :, 0], start=True, stop=True).then_inc(full, 1)
                elif name == "gvar":
                    pe.wait_ge(stats_ready, b * 2 + 2)
                    dst, full = take(u, name)
                    nc.tensor.matmul(dst[:, 0:CT], grp[:, :], gve[:, :], start=True, stop=True).then_inc(full, 1)
                else:
                    pe.wait_ge(w1e_ready, b + 1)
                    dst, full = take(u, name)
                    for c in range(CT):
                        last = nc.tensor.matmul(dst[:, 0:1], w1e[:, c, :], gmean[:, c:c + 1],
                                                start=(c == 0), stop=(c == CT - 1))
                    last.then_inc(full, 1)

            def front(u, b):
                for name in FRONT:
                    kind, j = name[0], int(name[1])
                    if kind == "c":
                        if j == 0:
                            for i in range(NCH):
                                pe.wait_ge(x_in[i], b * 16 + 16)
                        dst, full = take(u, name)
                        for hh in range(CHUNK // HALF):
                            for c in range(CT):
                                last = nc.tensor.matmul(dst[:, hh * HALF:(hh + 1) * HALF], w1e[:, c, :],
                                                        X[:, j, c, hh * HALF:(hh + 1) * HALF],
                                                        start=(c == 0), stop=(c == CT - 1))
                        last.then_inc(full, 1)
                    elif kind == "q":
                        pe.wait_ge(h1_ready, b * NCH + j + 1)
                        dst, full = take(u, name)
                        for hh in range(CHUNK // HALF):
                            last = nc.tensor.matmul(dst[0:QC, hh * HALF:(hh + 1) * HALF], wqT[:, :],
                                                    h1[:, j % 2, hh * HALF:(hh + 1) * HALF], start=True, stop=True)
                        last.then_inc(full, 1)
                    else:
                        dst, full = take(u, name)
                        for i in range(CHUNK // P):
                            last = nc.tensor.matmul(dst[:, i * KV:(i + 1) * KV], h1[:, j % 2, i * P:(i + 1) * P],
                                                    wkvT[:, :], start=True, stop=True)
                        last.then_inc(full, 1)

            def weights(u, i, yo):
                q, t = divmod(i, NT)
                dst, full = take(u, f"w{i}.{yo}")
                for xo in range(BX):
                    if t < NT - 1:
                        m = KWIN
                        e0 = EOFF + (t * TD - yo) * WX - xo
                        lhsT = Epad[:, e0:e0 + KWIN]
                    else:
                        m = KC
                        lhsT = Elast[:, yo * BX + xo, :]
                    x0 = q * XQ * BX + xo
                    last = nc.tensor.matmul(dst[0:m, xo * P:(xo + 1) * P], lhsT,
                                            Qv[:, :, :, yo, x0:x0 + BX + 1:BX],
                                            start=(xo % 4 == 0), stop=True, skip_group_check=True)
                last.then_inc(full, 1)

            def lam(u, b, with_stats):
                pe.wait_ge(*moved(f"q{NCH - 1}", b))
                pe.wait_ge(*moved(f"k{NCH - 1}", b))
                pe.wait_ge(sum_ready, b * (NCH * CT) + HEAD)
                pe.wait_ge(soft_ready, b + 1)
                dst, full = take(u, "cl")
                for i in range(PT):
                    last = nc.tensor.matmul(dst[0:DK, 0:DV], kS[:, i, :], vS[:, i, :],
                                            start=(i == 0), stop=(i == PT - 1))
                last.then_inc(full, 1)
                pe.wait_ge(q_in, b * (16 * len(SPLIT) * HEADS) + 16 * len(SPLIT) * HEADS)
                for yo in range(BY):
                    weights(u, 0, yo)
                for i in range(UNITS):
                    q, t = divmod(i, NT)
                    k = KWIN if t < NT - 1 else KC
                    pe.wait_ge(w_by_act, b * ((BY - 1) * UNITS) + (BY - 1) * (i + 1))
                    pe.wait_ge(w_by_dve, b * UNITS + i + 1)
                    if t == 0:
                        for xb in range(XQ * q, XQ * (q + 1)):
                            s = xb % SLOTS
                            per = 16 * (2 * TD + (TD if s == 0 else 0))
                            first = 16 * (TD + (TD if s == 0 else 0))
                            pe.wait_ge(v_in[s], b * per + (first if xb < SLOTS else per))
                    if i == NT - 1:
                        pe.wait_ge(content_in, b * (16 * SLOTS) + 16 * SLOTS)
                    for blk in range(NBLK):
                        if i < UNITS - 1 and blk in WGEN_AT:
                            weights(u, i + 1, WGEN_AT.index(blk))
                        bank, pos = divmod(blk, NBLK // 2)
                        if t == 0 and pos == 0:
                            pe.wait_ge(t_ready, b * (2 * NQ) + HEAD + max(2 * q - 1 + bank, 0))
                        yb, xbi = divmod(blk, XQ)
                        last = nc.tensor.matmul(acc[bank][:, pos * DV:(pos + 1) * DV], Wt[0:k, i % 2, blk, :],
                                                Vv[0:k, (XQ * q + xbi) % SLOTS, yb * BY + t * TD, :],
                                                start=(t == 0 and pos == 0), stop=(t == NT - 1),
                                                skip_group_check=True)
                        if pos == NBLK // 2 - 1:
                            last.then_inc(half_done, 1)
                    if with_stats and i in GN_AFTER:
                        gn_product(u, b + 1, GN_AFTER[i])

            def output(u, b):
                pe.wait_ge(h2_ready, b * (XQ * NQ) + HEAD + XQ * NQ)
                for j in range(NCH):
                    for t in range(CT):
                        dst, full = take(u, f"o{j}.{t}")
                        for hh in range(CHUNK // HALF):
                            n0 = j * CHUNK + hh * HALF
                            last = nc.tensor.matmul(dst[:, hh * HALF:(hh + 1) * HALF], w3T[:, t, :],
                                                    h2[:, n0:n0 + HALF], start=True, stop=True)
                        last.then_inc(full, 1)

            pe.wait_ge(setup_scaled, 1)
            pe.wait_ge(setup_pool, 3)
            for c in range(CT):
                nc.tensor.matmul(ring[0][:, c * P:(c + 1) * P], w1r[:, c * P:(c + 1) * P], ident[:, :],
                                 start=True, stop=True)
            for t in range(CT):
                nc.tensor.matmul(ring[0][:, HALF + t * P:HALF + (t + 1) * P], w3r[:, t, :], ident[:, :],
                                 start=True, stop=True)
            nc.tensor.matmul(ring[1][:, 0:QC], wqr, ident[0:QC, 0:QC], start=True, stop=True)
            nc.tensor.matmul(ring[1][:, QC:QC + KV], wkvr, ident[0:KV, 0:KV], start=True, stop=True)
            nc.tensor.matmul(ring[1][:, P:P + DV], vbb, ident[0:DV, 0:DV], start=True, stop=True).then_inc(setup_pe, 1)

            u = uses_before_loop()
            for name in GN_USES:
                gn_product(u, 0, name)
            front(u, 0)
            with pe.Fori(0, B - 1) as b:
                u = uses_in_loop(b)
                lam(u, b, True)
                front(u, b + 1)
                output(u, b)
            u = uses_after_loop()
            lam(u, B - 1, False)
            output(u, B - 1)

        def move_weights(engine_copy, u, i, yo):
            m = KWIN if i % NT < NT - 1 else KC
            src = ring[u.slot(f"w{i}.{yo}")][0:m, :].rearrange("m (xo h b) -> m h b xo", xo=BX, h=HEADS)
            dst = Wt[0:m, i % 2, :, :].rearrange("m b (h yo xo) -> m h b yo xo", h=HEADS, yo=BY)[:, :, :, yo, :]
            return engine_copy(dst, src)

        @block.scalar
        def _(act):
            def full(u, name):
                act.wait_ge(ring_full[u.slot(name)], u.full(name))
                return ring[u.slot(name)]

            def sqrt_of_var(b):
                act.wait_ge(gvar_ready, b + 1)
                nc.scalar.activation(gsq[:, :], gvar[:, :], ACT.Sqrt).then_inc(sqrt_done, 1)

            def front(u, b):
                for name in FRONT:
                    kind, j = name[0], int(name[1])
                    if kind == "c":
                        if j == 0:
                            act.wait_ge(nb1_ready, b + 1)
                        if j >= 2:
                            act.wait_ge(ring_full[u.slot(f"k{j - 2}")], u.full(f"k{j - 2}"))
                        src = full(u, name)
                        nc.scalar.activation(h1[:, j % 2, :], src[:, :], ACT.Relu, bias=nb1[:, 0:1])\
                            .then_inc(h1_ready, 1)
                    elif kind == "q":
                        src = full(u, name)
                        nc.scalar.activation(qp[:, 0, j * CHUNK:(j + 1) * CHUNK], src[0:QC, :], ACT.Identity,
                                             bias=pbi[0:QC, 2:3]).then_inc(qh_ready, 1)
                    else:
                        act.wait_ge(vs_ready, b * NCH + j + 1)
                        n = CHUNK // P
                        r0 = PAD + j * (CHUNK // W)
                        for odd in range(2):
                            nc.scalar.copy(vX[0:W, r0 + odd:r0 + odd + 2 * n - 1:2, :],
                                           vS[W * odd:W * (odd + 1), j * n:(j + 1) * n, :]).then_inc(vx_ready, 1)
                        act.wait_ge(r1_ready, b * NCH + j + 1)
                        nc.scalar.copy(qp[:, 1, j * CHUNK:(j + 1) * CHUNK], r1).then_inc(qm_done, 1)
                act.wait_ge(kmax_done, b + 1)
                nc.scalar.activation(kS[:, :, :], kS[:, :, :], ACT.Exp).then_inc(kexp_done, 1)

            def lam(u, b, with_stats):
                src = full(u, "cl")
                nc.scalar.copy(clS[:, :], src[0:DK, 0:DV]).then_inc(cl_ready, 1)

                def move(i):
                    for yo in range(BY):
                        if yo != VECTOR_YO:
                            full(u, f"w{i}.{yo}")
                            move_weights(nc.scalar.copy, u, i, yo).then_inc(w_by_act, 1)

                move(0)
                for i in range(UNITS):
                    if i < UNITS - 1:
                        move(i + 1)
                    q, t = divmod(i, NT)
                    if t == NT - 1:
                        act.wait_ge(t_ready, b * (2 * NQ) + HEAD + 2 * (q + 1))
                        Tv = T[:, :].rearrange("p (yb xb yo xo) -> p xb yb yo xo", xb=XQ, yo=BY, xo=BX)
                        for xbi in range(XQ):
                            x0 = (q * XQ + xbi) * BX
                            nc.scalar.activation(
                                h2v[:, :, x0:x0 + BX].rearrange("p (yb yo) xo -> p yb yo xo", yo=BY),
                                Tv[:, xbi], ACT.Relu,
                                bias=pbi[:, 1:2], scale=psc[:, 1:2]).then_inc(h2_ready, 1)
                    if with_stats and GN_AFTER.get(i) == "gvar":
                        sqrt_of_var(b + 1)

            act.sem_inc(h2_ready, HEAD)
            act.wait_ge(setup_dve, 1)
            nc.scalar.activation(psc[:, :], par[:, 3, :], ACT.Sqrt).then_inc(setup_act, 1)
            sqrt_of_var(0)
            front(uses_before_loop(), 0)
            with act.Fori(0, B - 1) as b:
                u = uses_in_loop(b)
                lam(u, b, True)
                front(u, b + 1)
            lam(uses_after_loop(), B - 1, False)

        @block.vector
        def _(dve):
            class Chain:
                def __init__(self, base):
                    self.base, self.n = base, 0

                def __call__(self, ins):
                    self.n += 1
                    ins.then_inc(dve_link, 1)
                    dve.wait_ge(dve_link, self.base + self.n)

            def full(u, name):
                dve.wait_ge(ring_full[u.slot(name)], u.full(name))
                return ring[u.slot(name)]

            def stats_part(b, n):
                j, hh = divmod(n, 2)
                if hh == 0:
                    dve.wait_ge(x_in[j], b * 16 + 16)
                for c in range(CT):
                    last = nc.vector.bn_stats(st[:, c, n, :], X[:, j, c, hh * HALF:(hh + 1) * HALF])
                return last

            def newton(chain, v, r, t):
                chain(nc.vector.tensor_tensor(t, r, r, ALU.mult))
                chain(nc.vector.tensor_tensor(t, t, v, ALU.mult))
                chain(nc.vector.tensor_scalar(t, t, -0.5, 1.5, ALU.mult, ALU.add))
                chain(nc.vector.tensor_tensor(r, r, t, ALU.mult))

            def gn_aggregate(chain, b, last):
                chain(last)
                nc.vector.memset(gtmp[:, :], 0.0)
                for c in range(CT):
                    done = nc.vector.bn_aggr(mv[:, c, :], st[:, c, :, :].rearrange("p a s -> p (a s)"))
                done.then_inc(stats_ready, 1)

            def gn_mean(chain, u, b):
                src = full(u, "gmean")
                nc.vector.tensor_copy(gmean[:, :], src[:, 0:CT]).then_inc(gmean_ready, 1)
                dve.wait_ge(gmean_ready, b + 1)
                chain(nc.vector.tensor_tensor(gtmp[:, :], mv[:, :, 0], gmean[:, :], ALU.subtract))
                chain(nc.vector.tensor_tensor(gtmp[:, :], gtmp[:, :], gtmp[:, :], ALU.mult))
                nc.vector.tensor_tensor(gve[:, :], gtmp[:, :], mv[:, :, 1], ALU.add).then_inc(stats_ready, 1)

            def gn_var(chain, u, b):
                src = full(u, "gvar")
                nc.vector.tensor_scalar(gvar[:, :], src[:, 0:CT], EPS, None, ALU.add).then_inc(gvar_ready, 1)
                dve.wait_ge(sqrt_done, b + 1)
                chain(nc.vector.reciprocal(rstd[:, :], gsq[:, :]))
                newton(chain, gvar[:, :], rstd[:, :], gtmp[:, :])
                for c in range(CT):
                    last = nc.vector.tensor_scalar(w1e[:, c, :], w1T[:, c, :], rstd[:, c:c + 1], None, ALU.mult)
                last.then_inc(w1e_ready, 1)
                chain(nc.vector.tensor_tensor(gtmp[:, :], gmean[:, :], rstd[:, :], ALU.mult))
                chain(nc.vector.tensor_tensor(bnew[:, :], pbi[:, 4:8], gtmp[:, :], ALU.subtract))

            def gn_bias(u, b):
                src = full(u, "bias1")
                nc.vector.tensor_tensor(nb1[:, :], pbi[:, 0:1], src[:, 0:1], ALU.subtract).then_inc(nb1_ready, 1)

            def keep_for_output(chain):
                chain(nc.vector.tensor_scalar(rcur[:, :], rstd[:, :], 1.0, None, ALU.add))
                chain(nc.vector.tensor_copy(bcur[:, :], bnew[:, :]))

            def front(chain, u, b):
                for name in FRONT:
                    kind, j = name[0], int(name[1])
                    if kind == "q":
                        src = full(u, name)
                        dve.wait_ge(qh_ready, b * NCH + j + 1)
                        dve.wait_ge(qparts_ready, b * NCH + j)
                        nc.vector.scalar_tensor_tensor(r1, src[0:QC, :], pbi[0:QC, 2:3],
                                                       qp[:, 0, j * CHUNK:(j + 1) * CHUNK],
                                                       ALU.add, ALU.subtract).then_inc(r1_ready, 1)
                    elif kind == "k":
                        src = full(u, name)
                        n = CHUNK // P
                        kv = src[:, 0:n * KV].rearrange("p (n c) -> p n c", c=KV)
                        last = nc.vector.tensor_copy(kS[:, j * n:(j + 1) * n, :], kv[:, :, DV:KV])
                        if j == NCH - 1:
                            chain(last)
                        nc.vector.tensor_tensor(vS[:, j * n:(j + 1) * n, :], kv[:, :, 0:DV],
                                                vbias[:, :].unsqueeze(1).to_broadcast([P, n, DV]),
                                                ALU.add).then_inc(vs_ready, 1)
                chain(nc.vector.reduce_max(kst[:, :], kS[:, :, :], AX_X))
                nc.vector.tensor_tensor(kS[:, :, :], kS[:, :, :],
                                        kst[:, :].unsqueeze(2).to_broadcast([P, PT, DK]),
                                        ALU.subtract).then_inc(kmax_done, 1)
                dve.wait_ge(kexp_done, b + 1)
                chain(nc.vector.reduce_sum(kst[:, :], kS[:, :, :], AX_X))
                chain(nc.vector.reciprocal(kst[:, :], kst[:, :]))
                nc.vector.tensor_tensor(kS[:, :, :], kS[:, :, :],
                                        kst[:, :].unsqueeze(2).to_broadcast([P, PT, DK]),
                                        ALU.mult).then_inc(soft_ready, 1)

            def lam(chain, u, b, with_stats):
                def move(i):
                    full(u, f"w{i}.{VECTOR_YO}")
                    move_weights(nc.vector.tensor_copy, u, i, VECTOR_YO).then_inc(w_by_dve, 1)

                move(0)
                for i in range(UNITS):
                    if i < UNITS - 1:
                        move(i + 1)
                    q, t = divmod(i, NT)
                    if t == NT - 1:
                        dve.wait_ge(h2_ready, b * (XQ * NQ) + HEAD + XQ * q)
                        for bank in range(2):
                            dve.wait_ge(half_done, b * (2 * UNITS) + 2 * i + bank + 1)
                            nc.vector.transpose(T[:, bank * HALF:(bank + 1) * HALF], acc[bank][:, :])\
                                .then_inc(t_ready, 1)
                    if with_stats and i in STAT_STEPS:
                        n = STAT_STEPS.index(i)
                        last = stats_part(b + 1, n)
                        if n == len(STAT_STEPS) - 1:
                            gn_aggregate(chain, b + 1, last)
                    if with_stats:
                        if GN_AFTER.get(i) == "gmean":
                            gn_mean(chain, u, b + 1)
                        if GN_AFTER.get(i) == "gvar":
                            gn_var(chain, u, b + 1)
                        if GN_AFTER.get(i) == "bias1":
                            gn_bias(u, b + 1)

            def output(u, b, split):
                dve.wait_ge(qparts_ready, split * NCH)
                for j in range(NCH):
                    dve.wait_ge(res_in[j], b * 16 + 16)
                    for t in range(CT):
                        src = full(u, f"o{j}.{t}")
                        nc.vector.scalar_tensor_tensor(T[:, :], X[:, j, t, :], rcur[:, t:t + 1], src[:, :],
                                                       ALU.mult, ALU.add).then_inc(sum_ready, 1)
                        dve.wait_ge(sum_ready, b * (NCH * CT) + HEAD + j * CT + t + 1)
                        nc.vector.scalar_tensor_tensor(X[:, j, t, :], T[:, :], bcur[:, t:t + 1], X[:, j, t, :],
                                                       ALU.add, ALU.max).then_inc(out_ready, 1)
                        dve.wait_ge(out_ready, b * (NCH * CT) + j * CT + t + 1)

            chain = Chain(0)
            dve.sem_inc(t_ready, HEAD)
            dve.sem_inc(sum_ready, HEAD)
            nc.vector.memset(vX[:, :, :], 0.0)
            nc.vector.memset(V[:, :, :], 0.0)
            chain(nc.vector.memset(Epad[:, :], 0.0))
            chain(nc.vector.memset(Elast[:, :, :], 0.0))
            dve.wait_ge(setup_in, N_SETUP_IN)
            g, be, m, v = (par[:, a, :] for a in range(4))
            nc.vector.tensor_scalar(v, v, EPS, None, ALU.add).then_inc(setup_dve, 1)
            dve.wait_ge(setup_act, 1)
            chain(nc.vector.reciprocal(g8[:, 0, :], psc[:, :]))
            newton(chain, v, g8[:, 0, :], g8[:, 1, :])
            chain(nc.vector.tensor_tensor(psc[:, :], g8[:, 0, :], g, ALU.mult))
            chain(nc.vector.tensor_tensor(g8[:, 2, :], m, psc[:, :], ALU.mult))
            chain(nc.vector.tensor_tensor(pbi[:, :], be, g8[:, 2, :], ALU.subtract))
            chain(nc.vector.tensor_scalar(w1r, w1r, psc[:, 0:1], None, ALU.mult))
            for t in range(CT):
                nc.vector.tensor_scalar(w3r[:, t, :], w3r[:, t, :], psc[:, 4 + t:5 + t], None, ALU.mult)
            nc.vector.tensor_scalar(wqr, wqr, psc[0:QC, 2:3], None, ALU.mult)
            chain(nc.vector.tensor_scalar(wkvr[0:DV, :], wkvr[0:DV, :], psc[0:DV, 3:4], None, ALU.mult))
            nc.vector.tensor_copy(vbb, pbi[0:DV, 3:4].to_broadcast([DV, P])).then_inc(setup_scaled, 1)
            chain(nc.vector.tensor_copy(epart[0], emb6))
            chain(nc.vector.tensor_tensor(eres, emb6, epart[0], ALU.subtract))
            nc.vector.tensor_copy(epart[1], eres).then_inc(setup_parts, 1)
            dve.wait_ge(setup_parts, 1)
            nc.vector.tensor_tensor(epart[2], eres, epart[1], ALU.subtract).then_inc(setup_parts, 2)
            dve.wait_ge(setup_pe, 1)
            nc.vector.tensor_copy(w1T[:, :, :].rearrange("p c n -> p (c n)"), ring[0][:, 0:HALF])
            nc.vector.tensor_copy(w3T[:, :, :].rearrange("p c n -> p (c n)"), ring[0][:, HALF:2 * HALF])
            nc.vector.tensor_copy(wqT[:, :], ring[1][:, 0:QC])
            nc.vector.tensor_copy(wkvT[:, :], ring[1][:, QC:QC + KV])
            chain(nc.vector.tensor_copy(vbias[:, :], ring[1][:, P:P + DV]))
            dve.wait_ge(setup_edma, 16 * len(SPLIT))
            chain(nc.vector.tensor_copy(Epad[:, EOFF:EOFF + R * WX].rearrange("p (a b) -> p a b", b=WX)[:, :, 0:R],
                                        Esel.rearrange("p (a b) -> p a b", a=R)))
            dve.wait_ge(setup_pool, 4)
            for yo in range(BY):
                for xo in range(BX):
                    e0 = EOFF + ((NT - 1) * TD - yo) * WX - xo
                    nc.vector.tensor_copy(Elast[:, yo * BX + xo, 0:LASTD * WX], Epad[:, e0:e0 + LASTD * WX])
            chain(nc.vector.tensor_copy(Elast[:, :, KWIN:KC], dlt.unsqueeze(1).to_broadcast([NE, PIX, DK])))
            u = uses_before_loop()
            for n in range(8):
                last = stats_part(0, n)
            gn_aggregate(chain, 0, last)
            gn_mean(chain, u, 0)
            gn_var(chain, u, 0)
            gn_bias(u, 0)
            keep_for_output(chain)
            front(chain, u, 0)
            pre = chain.n
            LOOP_LINKS = 16
            with dve.Fori(0, B - 1) as b:
                chain = Chain(b * LOOP_LINKS + pre)
                u = uses_in_loop(b)
                lam(chain, u, b, True)
                front(chain, u, b + 1)
                output(u, b, b + 2)
                keep_for_output(chain)
                assert chain.n == LOOP_LINKS, chain.n
            chain = Chain((B - 1) * LOOP_LINKS + pre)
            u = uses_after_loop()
            lam(chain, u, B - 1, False)
            output(u, B - 1, B)

        @block.gpsimd
        def _(pool):
            nc.gpsimd.memset(par[:, :, :], 1.0).then_inc(setup_pool, 1)
            nc.gpsimd.memset(ident[:, :], 0.0).then_inc(setup_pool, 1)
            pool.wait_ge(setup_pool, 2)
            nc.gpsimd.affine_select(out=ident[:, :], in_=ident[:, :], compare_op=ALU.not_equal, fill=1.0, base=0,
                                    pattern=[[-1, P]], channel_multiplier=1).then_inc(setup_pool, 1)
            nc.gpsimd.memset(dlt, 0.0).then_inc(setup_gp, 1)
            n = 1
            for g in range(NPART):
                pool.wait_ge(setup_gp, n)
                nc.gpsimd.affine_select(out=dlt, in_=dlt, compare_op=ALU.not_equal, fill=1.0, base=-g * DK,
                                        pattern=[[-1, DK]], channel_multiplier=1).then_inc(setup_gp, 1)
                n += 1
            nc.gpsimd.memset(grp[:, :], 1.0 / CPG).then_inc(setup_gp, 1)
            n += 1
            gv = grp[:, :].rearrange("p (a c) -> p a c", c=CPG)
            pool.wait_ge(setup_gp, n)
            nc.gpsimd.affine_select(out=gv, in_=gv, compare_op=ALU.is_ge, fill=0.0, base=0,
                                    pattern=[[-CPG, P // CPG], [0, CPG]], channel_multiplier=1).then_inc(setup_gp, 1)
            n += 1
            pool.wait_ge(setup_gp, n)
            nc.gpsimd.affine_select(out=gv, in_=gv, compare_op=ALU.is_ge, fill=0.0, base=CPG - 1,
                                    pattern=[[CPG, P // CPG], [0, CPG]], channel_multiplier=-1).then_inc(setup_pool, 1)

            def split_q(b):
                for j in range(NCH):
                    cols = slice(j * CHUNK, (j + 1) * CHUNK)
                    pool.wait_ge(qm_done, b * NCH + j + 1)
                    nc.gpsimd.tensor_tensor(qp[:, 2, cols], r1, qp[:, 1, cols], ALU.subtract)\
                        .then_inc(qparts_ready, 1)

            split_q(0)
            with pool.Fori(0, B - 1) as b:
                split_q(b + 1)


_IN = ["x"] + ["L0_conv_" + n for n in (
    "conv1_w bn1_g bn1_b bn1_m bn1_v q_w bnq_g bnq_b bnq_m bnq_v k_w v_w bnv_g bnv_b bnv_m bnv_v emb "
    "bn2_g bn2_b bn2_m bn2_v conv3_w bn3_g bn3_b bn3_m bn3_v").split()]


def kernel(**inputs):
    import numpy as np
    import concourse.bacc as bacc
    from concourse.bass_utils import run_bass_kernel_spmd

    nc = bacc.Bacc("TRN2", target_bir_lowering=False, num_devices=1, dynamic_dma_scratch_size=1024)
    arrays, ap = {}, {}
    for name in _IN:
        a = np.ascontiguousarray(inputs[name])
        arrays[name + "_dram"] = a
        ap[name.replace("L0_conv_", "")] = nc.dram_tensor(name + "_dram", a.shape, mybir.dt.from_np(a.dtype),
                                                          kind="ExternalInput").ap()
    out = nc.dram_tensor("out_dram", inputs["x"].shape, F32, kind="ExternalOutput").ap()
    bn = {n: [ap[f"bn{n}_{a}"] for a in "gbmv"] for n in ("1", "2", "3", "q", "v")}
    lambda_block(nc, ap["x"], ap["conv1_w"], bn["1"], ap["q_w"], bn["q"], ap["k_w"], ap["v_w"], bn["v"],
                 ap["emb"], bn["2"], ap["conv3_w"], bn["3"], out)
    got = run_bass_kernel_spmd(nc, [arrays], core_ids=[0])
    return got.results[0]["out_dram"]
```

```python
from contextlib import ExitStack

import concourse.bass as bass
from concourse import mybir

F32 = mybir.dt.float32
BF16 = mybir.dt.bfloat16
ALU = mybir.AluOpType
ACT = mybir.ActivationFunctionType
AX_X = mybir.AxisListType.X

P = 128
EPS = 1e-5
GROUPS = 32
R = 15
PAD = (R - 1) // 2
BY, BX = 8, 8
PIX = BY * BX
WY, WX = BY + R - 1, BX + R - 1
WIN = WY * WX
NT = 4
LASTW = WIN - (NT - 1) * P
NPART = 3
SPLIT = [(0, 0), (1, 0), (2, 0), (0, 1), (1, 1), (0, 2)]
CHUNK = 1024
STAT_STEPS = [4, 5, 6, 7, 9, 10, 11, 12]
GN_AFTER = {13: "gmean", 14: "gvar", 15: "bias1"}
ROWS = 2
PARTS = BY // ROWS
POOL_TILES = [1, 2, 4, 6, 8, 10, 12, 13]
H2_BESIDE = [[0, 1], [2], [3], []]
EXP_AFTER = 3
SUM_AFTER = 1
VECTOR_PART = 2
WGEN_AT = [0, 0, 1, 1]


def front_order():
    return ["c0", "c1", "q0", "k0", "c2", "q1", "k1", "c3", "q2", "k2", "q3", "k3"]


def lambda_order(with_stats):
    order = []
    for i in range(16):
        if i < 15:
            order += [f"w{i + 1}.{part}" for part in range(PARTS)]
        if with_stats and i in GN_AFTER:
            order.append(GN_AFTER[i])
    return order


LEAD = [f"w0.{part}" for part in range(PARTS)] + ["cl"]
LEAD_AT = {11: 1, 13: 1, 14: 1, 15: 2}


def output_order(with_lead):
    order, lead = [], list(LEAD)
    for n in range(16):
        order.append(f"o{n // 4}.{n % 4}")
        for _ in range(LEAD_AT.get(n, 0) if with_lead else 0):
            order.append(lead.pop(0))
    return order


def lambda_block(nc, x, w1, bn1, wq, bnq, wk, wv, bnv, emb, bn2, w3, bn3, out):
    B, C, H, W = x.shape
    N = H * W
    CT = C // P
    MID = w1.shape[0]
    QC = wq.shape[0]
    DK = wk.shape[0]
    DV = wv.shape[0]
    HEADS = QC // DK
    KV = DV + DK
    NCH = N // CHUNK
    HALF = 512
    NBY, NXB = H // BY, W // BX
    XQ = 2
    NQ = NXB // XQ
    NBLK = NBY * XQ
    UNITS = NQ * NT
    COLS = 4
    GROUPED = NBLK // COLS
    assert COLS * DV == P and GROUPED * HEADS * PIX == 2 * HALF
    assert MID == P and HEADS * DV == P and DV == 32 and NCH == 4 and CT == 4 and NQ == 4
    XM = (H + 2 * PAD + BY - 1) // BY
    WPAD = W + 2 * PAD
    PT = N // P
    CPG = C // GROUPS
    KC = LASTW + DK
    ECOLS = WX + BX
    EOFF = BX * WY

    xv = x.rearrange("b (c p) h w -> b p c (h w)", p=P)
    ov = out.rearrange("b (c p) h w -> b p c (h w)", p=P)

    ctx = ExitStack()
    with ctx:
        def sb(name, shape, dt=F32):
            return ctx.enter_context(nc.sbuf_tensor(name, shape, dt))

        def sem(name):
            return ctx.enter_context(nc.semaphore(name))

        X = sb("X", [P, NCH, CT, CHUNK])
        region = sb("region", [P, 2 * NBLK * HEADS * PIX])
        Q = sb("Q", [len(SPLIT) * DK, HEADS, N], BF16)
        h2 = sb("h2", [P, N])
        sums = sb("sums", [P, 2, HEADS, GROUPED, PIX])
        hD = nc.dram_tensor("lambda_sums", (NQ, COLS, DV, HEADS, GROUPED * PIX), F32, kind="Internal").ap()
        V = sb("V", [P, NT, NXB, NBY * DV])
        vX = sb("vX", [W, BY, XM, DV])
        vD = nc.dram_tensor("v_windows", (WPAD, WY, NBY * DV), F32, kind="Internal").ap()
        kS = sb("kS", [P, PT, DK])
        w1T = sb("w1T", [P, CT, MID])
        w1e = sb("w1e", [P, CT, MID])
        w3T = sb("w3T", [P, CT, P])
        wqT = sb("wqT", [P, QC])
        wkvT = sb("wkvT", [P, KV])
        grp = sb("grp", [P, P])
        ident = sb("ident", [P, P])
        qD = nc.dram_tensor("q_parts", (QC, NPART, N), BF16, kind="Internal").ap()
        Epad = sb("Epad", [len(SPLIT) * DK, ECOLS * WY], BF16)
        Elast = sb("Elast", [len(SPLIT) * DK, PIX, P], BF16)
        vbias = sb("vbias", [P, DV])
        st = sb("st", [P, CT, 2 * NCH, 6])
        mv = sb("mv", [P, CT, 2])
        par = sb("par", [P, 4, 8])
        psc = sb("psc", [P, 8])
        pbi = sb("pbi", [P, 8])
        g8 = sb("g8", [P, 4, 8])
        gmean = sb("gmean", [P, CT])
        gtmp = sb("gtmp", [P, CT])
        gve = sb("gve", [P, CT])
        gvar = sb("gvar", [P, CT])
        gsq = sb("gsq", [P, CT])
        rstd = sb("rstd", [P, CT])
        bnew = sb("bnew", [P, CT])
        rcur = sb("rcur", [P, CT])
        r1cur = sb("r1cur", [P, CT])
        bcur = sb("bcur", [P, CT])
        nb1 = sb("nb1", [P, 1])
        kst = sb("kst", [P, PT])
        clS = sb("clS", [DK, DV])
        zeros = sb("zeros", [DK, DV])

        Wt = region[:, :].rearrange("p (u b n) -> p u b n", u=2, n=HEADS * PIX)
        h1 = region[:, 0:2 * CHUNK].rearrange("p (u n) -> p u n", u=2)
        q0 = region[0:QC, 2 * CHUNK:2 * CHUNK + N // 2].bitcast(BF16)
        q12 = region[QC:2 * QC, 2 * CHUNK:2 * CHUNK + N].bitcast(BF16).rearrange("p (a n) -> p a n", a=2)
        r1 = region[QC:2 * QC, 2 * CHUNK + N:4 * CHUNK + N].rearrange("p (u n) -> p u n", u=2)
        Qv = Q[:, :, :].rearrange("p h (yb yo xb xo) -> p h xb yb yo xo", yo=BY, xb=NXB, xo=BX)
        T = sums[:, 0, :, :, :].rearrange("p h i n -> p (h i n)")
        vS = sums[:, 1, :, :, :].rearrange("p h i n -> p (h i n)").rearrange("p (n c) -> p n c", c=DV)
        h2v = h2[:, :].rearrange("p (xb yb yo xo) -> p yb yo xb xo", xb=NXB, yb=NBY, yo=BY)
        h2g = h2[:, :].rearrange("p (q c n) -> p q c n", q=NQ, c=COLS)
        Vv = V[:, :, :, :].rearrange("p t xb (yb v) -> p t xb yb v", v=DV)
        o = 0
        w1r = region[:, o:o + C]; o += C
        w3r = region[:, o:o + CT * P].rearrange("p (t n) -> p t n", t=CT); o += CT * P
        wqr = region[0:QC, o:o + MID]; o += MID
        wkvr = region[0:KV, o:o + MID]; o += MID
        vbb = region[0:DV, o:o + P]; o += P
        NE = len(SPLIT) * DK
        RR = R * R
        emb6 = region[0:NE, o:o + RR]; o += RR
        eres = region[0:NE, o:o + RR]; o += RR
        epart = [region[0:NE, o + 128 * a:o + 128 * a + 128].bitcast(BF16)[:, 0:RR] for a in range(NPART)]
        o += NPART * 128
        dlt = region[0:NE, o:o + DK]; o += DK
        Esel = region[0:NE, o:o + 128].bitcast(BF16)[:, 0:RR]; o += 128

        ring = [ctx.enter_context(nc.psum_tensor(f"ring{i}", [P, CHUNK], F32)) for i in range(3)]
        acc = [ctx.enter_context(nc.psum_tensor(f"acc{i}", [P, HALF], F32)) for i in range(2)]

        setup_in = sem("setup_in")
        setup_dve = sem("setup_dve")
        setup_pool = sem("setup_pool")
        setup_act = sem("setup_act")
        setup_gp = sem("setup_gp")
        setup_scaled = sem("setup_scaled")
        setup_pe = sem("setup_pe")
        setup_edma = sem("setup_edma")
        setup_parts = sem("setup_parts")
        ring_full = [sem(f"ring_full{i}") for i in range(3)]
        x_in = [sem(f"x_in{j}") for j in range(NCH)]
        res_in = [sem(f"res_in{j}") for j in range(NCH)]
        out_done = [sem(f"out_done{j}") for j in range(NCH)]
        stats_ready = sem("stats_ready")
        gmean_ready = sem("gmean_ready")
        whole_sum = sem("whole_sum")
        half_sum = sem("half_sum")
        gvar_ready = sem("gvar_ready")
        sqrt_done = sem("sqrt_done")
        w1e_ready = sem("w1e_ready")
        nb1_ready = sem("nb1_ready")
        h1_ready = sem("h1_ready")
        qh_ready = sem("qh_ready")
        r1_ready = sem("r1_ready")
        qm_done = sem("qm_done")
        qparts_ready = sem("qparts_ready")
        q_in = sem("q_in")
        vs_ready = sem("vs_ready")
        vx_ready = sem("vx_ready")
        kmax_done = sem("kmax_done")
        kexp_done = sem("kexp_done")
        soft_ready = sem("soft_ready")
        cl_ready = sem("cl_ready")
        content_ready = sem("content_ready")
        q_out = sem("q_out")
        v_out = sem("v_out")
        v_in = sem("v_in")
        setup_vd = sem("setup_vd")
        setup_zero = sem("setup_zero")
        half_relu = sem("half_relu")
        pool_out = sem("pool_out")
        w_by_act = sem("w_by_act")
        w_by_dve = sem("w_by_dve")
        half_done = sem("half_done")
        sums_out = [sem(f"sums_out{i}") for i in range(2)]
        h_stored = [sem(f"h_stored{i}") for i in range(2)]
        h_in = sem("h_in")
        h2_ready = sem("h2_ready")
        out_ready = sem("out_ready")
        dve_link = sem("dve_link")

        HEAD = 1

        N_VOUT = -(-WY // BY)
        VEC_TILES = [n for n in range(NCH * CT) if n not in POOL_TILES]
        W_ACT = (PARTS - 1) * UNITS + 1
        NPOOL, NVEC = len(POOL_TILES), len(VEC_TILES)
        GN_USES = ["gmean", "gvar", "bias1"]
        FRONT = front_order()
        LAM = lambda_order(True)
        LAM_END = lambda_order(False)
        OUT = output_order(True)
        OUT_END = output_order(False)
        FIRST = len(GN_USES + FRONT + LEAD)
        PER = len(LAM) + len(FRONT) + len(OUT)
        assert PER % 3 == 0

        class Uses:
            def __init__(self, order, start, it):
                self.order, self.it = order, it
                self.at = {name: n for n, (name, _b) in enumerate(order)}
                self.start = start

            def slot(self, name):
                return (self.start + self.at[name]) % 3

            def full(self, name):
                return self.it * (PER // 3) + (self.start + self.at[name]) // 3 + 1

            def before(self, name):
                n = self.at[name] - 3
                return self.order[n] if n >= 0 else None

        def moved(name, b):
            if name == "cl":
                return cl_ready, b + 1
            if name in GN_USES:
                return {"gmean": gmean_ready, "gvar": gvar_ready, "bias1": nb1_ready}[name], b + 1
            kind = name[0]
            if kind == "w":
                i, part = (int(a) for a in name[1:].split("."))
                if i == 0:
                    return w_by_act, b * W_ACT + part + 1
                if part == VECTOR_PART:
                    return w_by_dve, b * (UNITS - 1) + i
                before = part if part < VECTOR_PART else part - 1
                return w_by_act, b * W_ACT + (PARTS - 1) * i + before + 2
            if kind == "o":
                j, t = (int(a) for a in name[1:].split("."))
                n = j * CT + t
                if n in POOL_TILES:
                    return half_sum, b * NPOOL + HEAD + POOL_TILES.index(n) + 1
                return whole_sum, b * NVEC + HEAD + VEC_TILES.index(n) + 1
            return {"c": h1_ready, "q": r1_ready, "k": vs_ready}[kind], b * NCH + int(name[1]) + 1

        def images(order, b):
            return [(name, b) for name in order]

        def uses_before_loop():
            return Uses(images(GN_USES + FRONT + LEAD, 0), 0, 0)

        def uses_in_loop(b):
            order = [(name, b + 1 if name in GN_USES else b) for name in LAM] + images(FRONT, b + 1)
            return Uses(order + [(name, b + 1 if name in LEAD else b) for name in OUT], FIRST, b)

        def uses_after_loop():
            return Uses(images(LAM_END + OUT_END, B - 1), FIRST, B - 1)

        block = ctx.enter_context(nc.Block())

        @block.sync
        def _(sp):
            def load_x(b, j):
                sp.dma_start(X[:, j, :, :], xv[b, :, :, j * CHUNK:(j + 1) * CHUNK]).then_inc(x_in[j], 16)

            def store_q(b, j):
                sp.wait_ge(qparts_ready, b * NCH + j + 1)
                cols = slice(j * CHUNK, (j + 1) * CHUNK)
                sp.dma_start(qD[:, 0, cols], q0[:, cols]).then_inc(q_out, 16)
                sp.dma_start(qD[:, 1:NPART, cols], q12[:, :, cols]).then_inc(q_out, 16)

            def spread(b):
                sp.wait_ge(vx_ready, b * BY + BY)
                for a in range(0, WY, BY):
                    n = min(BY, WY - a)
                    sp.dma_start(vD[PAD:PAD + W, a:a + n, :],
                                 vX[:, 0:n, a // BY:a // BY + NBY, :].rearrange("x r m v -> x r (m v)"))\
                        .then_inc(v_out, 16)
                sp.wait_ge(q_out, b * (32 * NCH) + 32 * NCH)
                for g, (a, _e) in enumerate(SPLIT):
                    sp.dma_start(Q[g * DK:(g + 1) * DK, :, :],
                                 qD[:, a, :].rearrange("(h k) n -> k h n", k=DK)).then_inc(q_in, 16)
                sp.wait_ge(v_out, b * (16 * N_VOUT) + 16 * N_VOUT)
                row = NBY * DV
                for t in range(NT):
                    n = P if t < NT - 1 else LASTW
                    p0 = 0 if t < NT - 1 else DK
                    src = bass.AP(vD.tensor, t * P * row, [[row, n], [BX * WY * row, NXB], [1, row]])
                    sp.dma_start(V[p0:p0 + n, t, :, :], src).then_inc(v_in, 16)

            def read_sums(b, q):
                sp.wait_ge(h_stored[q % 2], b * (8 * NQ) + 16 * (q // 2 + 1))
                for h in range(HEADS):
                    sp.dma_start(h2g[h * DV:(h + 1) * DV, q, :, :],
                                 hD[q, :, :, h, :].rearrange("c v n -> v c n")).then_inc(h_in, 16)

            def during_lambda(b, last):
                if not last:
                    for j in range(NCH):
                        sp.wait_ge(out_done[j], b * (16 * CT) + HEAD)
                        load_x(b + 1, j)
                for q in range(NQ):
                    for i in range(2):
                        sp.wait_ge(sums_out[i], b * NQ + HEAD + q + 1)
                    sp.dma_start(hD[q].rearrange("c v h n -> (c v) (h n)"),
                                 sums[:, q % 2, :, :, :].rearrange("p h i n -> p (h i n)")).then_inc(h_stored[q % 2], 16)
                    if q:
                        read_sums(b, q - 1)
                read_sums(b, NQ - 1)

            def during_output(b):
                for j in range(NCH):
                    for t in range(CT):
                        n = j * CT + t
                        if n in POOL_TILES:
                            sp.wait_ge(pool_out, b * NPOOL + HEAD + POOL_TILES.index(n) + 1)
                        else:
                            sp.wait_ge(out_ready, b * NVEC + VEC_TILES.index(n) + 1)
                        sp.dma_start(ov[b, :, t, j * CHUNK:(j + 1) * CHUNK],
                                     X[:, j, t, :]).then_inc(out_done[j], 16)

            def reload(b, j):
                sp.dma_start(X[:, j, :, :], xv[b, :, :, j * CHUNK:(j + 1) * CHUNK]).then_inc(res_in[j], 16)

            for j in range(NCH):
                sp.sem_inc(out_done[j], HEAD)
                load_x(0, j)
            sp.dma_start(w1r, w1).then_inc(setup_in, 16)
            sp.dma_start(w3r, w3.rearrange("(t p) c -> p t c", p=P)).then_inc(setup_in, 16)
            sp.dma_start(wqr, wq).then_inc(setup_in, 16)
            sp.dma_start(wkvr[0:DV, :], wv).then_inc(setup_in, 16)
            sp.dma_start(wkvr[DV:KV, :], wk).then_inc(setup_in, 16)
            for g in range(len(SPLIT)):
                sp.dma_start(emb6[g * DK:(g + 1) * DK, :], emb.rearrange("k a b -> k (a b)")).then_inc(setup_in, 16)
            sp.wait_ge(setup_pool, 1)
            for n, (bn, size) in enumerate([(bn1, MID), (bn2, P), (bnq, QC), (bnv, DV)]):
                for a in range(4):
                    sp.dma_start(par[0:size, a, n:n + 1],
                                 bn[a].rearrange("(p a) -> p a", a=1)).then_inc(setup_in, 16)
            for a in range(4):
                for t in range(CT):
                    sp.dma_start(par[:, a, 4 + t:5 + t],
                                 bn3[a][t * P:(t + 1) * P].rearrange("(p a) -> p a", a=1)).then_inc(setup_in, 16)
            sp.wait_ge(setup_parts, 3)
            for g, (_a, e) in enumerate(SPLIT):
                sp.dma_start(Esel[g * DK:(g + 1) * DK, :], epart[e][g * DK:(g + 1) * DK, :]).then_inc(setup_edma, 16)

            sp.wait_ge(setup_zero, 1)
            for x0 in (0, PAD + W):
                for a in range(0, WY, BY):
                    n = min(BY, WY - a)
                    sp.dma_start(vD[x0:x0 + PAD, a:a + n, :],
                                 vX[0:PAD, 0:n, 0:NBY, :].rearrange("x r m v -> x r (m v)")).then_inc(setup_vd, 16)
            sp.wait_ge(setup_vd, 2 * N_VOUT * 16)
            for j in range(NCH):
                store_q(0, j)
            spread(0)
            with sp.Fori(0, B - 1) as b:
                u = uses_in_loop(b)
                during_lambda(b, False)
                for name in FRONT:
                    j = int(name[1])
                    if name[0] == "c":
                        sp.wait_ge(ring_full[u.slot(name)], u.full(name))
                        reload(b, j)
                    if name[0] == "k":
                        store_q(b + 1, j)
                spread(b + 1)
                during_output(b)
            e = B - 1
            during_lambda(e, True)
            for j in range(NCH):
                sp.wait_ge(out_done[j], e * (16 * CT) + HEAD)
                reload(e, j)
            during_output(e)
            for j in range(NCH):
                sp.wait_ge(out_done[j], B * 16 * CT + HEAD)

        N_SETUP_IN = 16 * (5 + len(SPLIT) + 16 + 4 * CT)

        @block.tensor
        def _(pe):
            def take(u, name):
                s = u.slot(name)
                prior = u.before(name)
                if prior:
                    pe.wait_ge(*moved(*prior))
                return ring[s], ring_full[s]

            def gn_product(u, b, name):
                if name == "gmean":
                    pe.wait_ge(stats_ready, b * 2 + 1)
                    dst, full = take(u, name)
                    nc.tensor.matmul(dst[:, 0:CT], grp[:, :], mv[:, :, 0], start=True, stop=True).then_inc(full, 1)
                elif name == "gvar":
                    pe.wait_ge(stats_ready, b * 2 + 2)
                    dst, full = take(u, name)
                    nc.tensor.matmul(dst[:, 0:CT], grp[:, :], gve[:, :], start=True, stop=True).then_inc(full, 1)
                else:
                    pe.wait_ge(w1e_ready, b + 1)
                    dst, full = take(u, name)
                    for c in range(CT):
                        last = nc.tensor.matmul(dst[:, 0:1], w1e[:, c, :], gmean[:, c:c + 1],
                                                start=(c == 0), stop=(c == CT - 1))
                    last.then_inc(full, 1)

            def front(u, b):
                for name in FRONT:
                    kind, j = name[0], int(name[1])
                    if kind == "c":
                        if j == 0:
                            for i in range(NCH):
                                pe.wait_ge(x_in[i], b * 16 + 16)
                        dst, full = take(u, name)
                        for hh in range(CHUNK // HALF):
                            for c in range(CT):
                                last = nc.tensor.matmul(dst[:, hh * HALF:(hh + 1) * HALF], w1e[:, c, :],
                                                        X[:, j, c, hh * HALF:(hh + 1) * HALF],
                                                        start=(c == 0), stop=(c == CT - 1))
                        last.then_inc(full, 1)
                    elif kind == "q":
                        pe.wait_ge(h1_ready, b * NCH + j + 1)
                        dst, full = take(u, name)
                        for hh in range(CHUNK // HALF):
                            last = nc.tensor.matmul(dst[0:QC, hh * HALF:(hh + 1) * HALF], wqT[:, :],
                                                    h1[:, j % 2, hh * HALF:(hh + 1) * HALF], start=True, stop=True)
                        last.then_inc(full, 1)
                    else:
                        dst, full = take(u, name)
                        for i in range(CHUNK // P):
                            last = nc.tensor.matmul(dst[:, i * KV:(i + 1) * KV], h1[:, j % 2, i * P:(i + 1) * P],
                                                    wkvT[:, :], start=True, stop=True)
                        last.then_inc(full, 1)

            def weights(u, i, part):
                q, t = divmod(i, NT)
                dst, full = take(u, f"w{i}.{part}")
                n = HEADS * NBLK
                for k in range(ROWS * BX):
                    yo, xo = part * ROWS + k // BX, k % BX
                    if t < NT - 1:
                        e0 = EOFF + t * P - xo * WY - yo
                        lhsT = Epad[:, e0:e0 + P]
                    else:
                        lhsT = Elast[:, yo * BX + xo, :]
                    last = nc.tensor.matmul(dst[:, k * n:(k + 1) * n], lhsT,
                                            Qv[:, :, XQ * q:XQ * (q + 1), :, yo, xo],
                                            start=(k * n % HALF == 0), stop=True, skip_group_check=True)
                last.then_inc(full, 1)

            def lead(u, b, name):
                if name == "cl":
                    pe.wait_ge(soft_ready, b * NCH + NCH)
                    dst, full = take(u, name)
                    for i in range(PT):
                        last = nc.tensor.matmul(dst[0:DK, 0:DV], kS[:, i, :], vS[:, i, :],
                                                start=(i == 0), stop=(i == PT - 1))
                    last.then_inc(full, 1)
                else:
                    if name == LEAD[0]:
                        pe.wait_ge(q_in, b * (16 * len(SPLIT)) + 16 * len(SPLIT))
                    weights(u, 0, LEAD.index(name))

            def lam(u, b, with_stats):
                pe.wait_ge(whole_sum, b * NVEC + HEAD)
                pe.wait_ge(cl_ready, b + 1)
                pe.wait_ge(v_in, b * (16 * NT) + 16 * NT)
                for i in range(UNITS):
                    q, t = divmod(i, NT)
                    k = P if t < NT - 1 else KC
                    pe.wait_ge(w_by_act, b * W_ACT + (PARTS - 1) * (i + 1) + 1)
                    if i:
                        pe.wait_ge(w_by_dve, b * (UNITS - 1) + i)
                    if i == NT - 1:
                        pe.wait_ge(content_ready, b + 1)
                    for g in range(GROUPED):
                        if i < UNITS - 1:
                            for part in range(PARTS):
                                if WGEN_AT[part] == g:
                                    weights(u, i + 1, part)
                        bank, half = divmod(g, 2)
                        if t == 0 and half == 0:
                            pe.wait_ge(sums_out[bank], b * NQ + HEAD + q)
                        for c in range(COLS):
                            xbi, yb = divmod(c * GROUPED + g, NBY)
                            last = nc.tensor.matmul(acc[bank][c * DV:(c + 1) * DV, half * HEADS * PIX:
                                                              (half + 1) * HEADS * PIX],
                                                    Vv[0:k, t, XQ * q + xbi, yb, :],
                                                    Wt[0:k, (i + 1) % 2, c * GROUPED + g, :],
                                                    start=(t == 0 and half == 0), stop=(t == NT - 1),
                                                    skip_group_check=True)
                        if half == 1:
                            last.then_inc(half_done, 1)
                    if with_stats and i in GN_AFTER:
                        gn_product(u, b + 1, GN_AFTER[i])

            def output(u, b, order):
                pe.wait_ge(h2_ready, b * NCH + NCH)
                for name in order:
                    if name in LEAD:
                        lead(u, b + 1, name)
                        continue
                    j, t = (int(a) for a in name[1:].split("."))
                    dst, full = take(u, name)
                    for hh in range(CHUNK // HALF):
                        yb = (j * CHUNK + hh * HALF) // (BY * W)
                        last = nc.tensor.matmul(dst[:, hh * HALF:(hh + 1) * HALF], w3T[:, t, :],
                                                h2v[:, yb, :, :, :], start=True, stop=True)
                    last.then_inc(full, 1)

            pe.wait_ge(setup_scaled, 1)
            pe.wait_ge(setup_pool, 3)
            for c in range(CT):
                nc.tensor.matmul(ring[0][:, c * P:(c + 1) * P], w1r[:, c * P:(c + 1) * P], ident[:, :],
                                 start=True, stop=True)
            for t in range(CT):
                nc.tensor.matmul(ring[0][:, HALF + t * P:HALF + (t + 1) * P], w3r[:, t, :], ident[:, :],
                                 start=True, stop=True)
            nc.tensor.matmul(ring[1][:, 0:QC], wqr, ident[0:QC, 0:QC], start=True, stop=True)
            nc.tensor.matmul(ring[1][:, QC:QC + KV], wkvr, ident[0:KV, 0:KV], start=True, stop=True)
            nc.tensor.matmul(ring[1][:, P:P + DV], vbb, ident[0:DV, 0:DV], start=True, stop=True).then_inc(setup_pe, 1)

            u = uses_before_loop()
            for name in GN_USES:
                gn_product(u, 0, name)
            front(u, 0)
            for name in LEAD:
                lead(u, 0, name)
            with pe.Fori(0, B - 1) as b:
                u = uses_in_loop(b)
                lam(u, b, True)
                front(u, b + 1)
                output(u, b, OUT)
            u = uses_after_loop()
            lam(u, B - 1, False)
            output(u, B - 1, OUT_END)

        def move_weights(engine_copy, u, i, part):
            m = P if i % NT < NT - 1 else KC
            n = ROWS * BX
            src = ring[u.slot(f"w{i}.{part}")][0:m, :].rearrange("m (k h b) -> m h b k", k=n, h=HEADS)
            dst = Wt[0:m, (i + 1) % 2, :, :].rearrange("m b (h y k) -> m h b y k", h=HEADS, k=n)[:, :, :, part, :]
            return engine_copy(dst, src)

        def move_sums(engine_copy, q, bank):
            src = acc[bank][:, :].rearrange("p (i h n) -> p h i n", i=2, h=HEADS)
            return engine_copy(sums[:, q % 2, :, 2 * bank:2 * bank + 2, :], src)

        @block.scalar
        def _(act):
            def full(u, name):
                act.wait_ge(ring_full[u.slot(name)], u.full(name))
                return ring[u.slot(name)]

            def sqrt_of_var(b):
                act.wait_ge(gvar_ready, b + 1)
                nc.scalar.activation(gsq[:, :], gvar[:, :], ACT.Sqrt).then_inc(sqrt_done, 1)

            def bn2_relu(b, j):
                if j == 0:
                    act.wait_ge(h_in, b * (16 * HEADS * NQ) + 16 * HEADS * NQ)
                part = h2[:, j * CHUNK:(j + 1) * CHUNK]
                nc.scalar.activation(part, part, ACT.Relu, bias=pbi[:, 1:2], scale=psc[:, 1:2]).then_inc(h2_ready, 1)

            def front(u, b, with_h2):
                for name in FRONT:
                    kind, j = name[0], int(name[1])
                    if kind == "c":
                        if j == 0:
                            act.wait_ge(nb1_ready, b + 1)
                        if j >= 2:
                            act.wait_ge(ring_full[u.slot(f"k{j - 2}")], u.full(f"k{j - 2}"))
                        src = full(u, name)
                        nc.scalar.activation(h1[:, j % 2, :], src[:, :], ACT.Relu, bias=nb1[:, 0:1])\
                            .then_inc(h1_ready, 1)
                    elif kind == "q":
                        src = full(u, name)
                        nc.scalar.activation(q0[:, j * CHUNK:(j + 1) * CHUNK], src[0:QC, :], ACT.Identity,
                                             bias=pbi[0:QC, 2:3]).then_inc(qh_ready, 1)
                    else:
                        act.wait_ge(r1_ready, b * NCH + j + 1)
                        nc.scalar.copy(q12[:, 0, j * CHUNK:(j + 1) * CHUNK], r1[:, j % 2, :]).then_inc(qm_done, 1)
                        if j:
                            softmax_exp(b, j - 1)
                        if with_h2:
                            for part in H2_BESIDE[j]:
                                bn2_relu(b - 1, part)
                act.wait_ge(vs_ready, b * NCH + NCH)
                for r in range(BY):
                    m0 = 0 if r >= PAD else 1
                    y0 = m0 * BY + r - PAD
                    odd = y0 % 2
                    nc.scalar.copy(vX[:, r, m0:m0 + NBY, :],
                                   vS[W * odd:W * (odd + 1), y0 // 2:PT:BY // 2, :]).then_inc(vx_ready, 1)
                    if r == EXP_AFTER:
                        softmax_exp(b, NCH - 1)

            def softmax_exp(b, j):
                cols = slice(j * (CHUNK // P), (j + 1) * (CHUNK // P))
                act.wait_ge(kmax_done, b * NCH + j + 1)
                nc.scalar.activation(kS[:, cols, :], kS[:, cols, :], ACT.Exp).then_inc(kexp_done, 1)

            def lead(u, name):
                src = full(u, name)
                if name == "cl":
                    nc.scalar.copy(clS[:, :], src[0:DK, 0:DV]).then_inc(cl_ready, 1)
                else:
                    move_weights(nc.scalar.copy, u, 0, LEAD.index(name)).then_inc(w_by_act, 1)

            def lam(u, b, with_stats):
                act.wait_ge(pool_out, b * NPOOL + HEAD)

                def move(i):
                    for part in range(PARTS):
                        if part != VECTOR_PART:
                            full(u, f"w{i}.{part}")
                            move_weights(nc.scalar.copy, u, i, part).then_inc(w_by_act, 1)

                for i in range(UNITS):
                    if i < UNITS - 1:
                        move(i + 1)
                    q, t = divmod(i, NT)
                    if t == NT - 1:
                        act.wait_ge(half_done, b * (2 * UNITS) + 2 * i + 1)
                        if q >= 2:
                            act.wait_ge(h_stored[q % 2], b * (8 * NQ) + 16 * (q // 2))
                        move_sums(nc.scalar.copy, q, 0).then_inc(sums_out[0], 1)
                    if with_stats and GN_AFTER.get(i) == "gvar":
                        sqrt_of_var(b + 1)

            def output(u, b, order):
                for name in order:
                    if name in LEAD:
                        lead(u, name)
                        continue
                    j, t = (int(a) for a in name[1:].split("."))
                    if j * CT + t in POOL_TILES:
                        i = POOL_TILES.index(j * CT + t)
                        act.wait_ge(half_sum, b * NPOOL + HEAD + i + 1)
                        nc.scalar.activation(h1[:, i % 2, :], h1[:, i % 2, :], ACT.Relu,
                                             bias=bcur[:, t:t + 1]).then_inc(half_relu, 1)

            act.sem_inc(sums_out[0], HEAD)
            act.wait_ge(setup_dve, 1)
            nc.scalar.activation(psc[:, :], par[:, 3, :], ACT.Sqrt).then_inc(setup_act, 1)
            sqrt_of_var(0)
            act.wait_ge(setup_vd, 2 * N_VOUT * 16)
            u = uses_before_loop()
            front(u, 0, False)
            for name in LEAD:
                lead(u, name)
            with act.Fori(0, B - 1) as b:
                u = uses_in_loop(b)
                lam(u, b, True)
                front(u, b + 1, True)
                output(u, b, OUT)
            u = uses_after_loop()
            lam(u, B - 1, False)
            for j in range(NCH):
                bn2_relu(B - 1, j)
            output(u, B - 1, OUT_END)

        @block.vector
        def _(dve):
            class Chain:
                def __init__(self, base):
                    self.base, self.n = base, 0

                def __call__(self, ins):
                    self.n += 1
                    ins.then_inc(dve_link, 1)
                    dve.wait_ge(dve_link, self.base + self.n)

            def full(u, name):
                dve.wait_ge(ring_full[u.slot(name)], u.full(name))
                return ring[u.slot(name)]

            def stats_part(b, n):
                j, hh = divmod(n, 2)
                if hh == 0:
                    dve.wait_ge(x_in[j], b * 16 + 16)
                for c in range(CT):
                    last = nc.vector.bn_stats(st[:, c, n, :], X[:, j, c, hh * HALF:(hh + 1) * HALF])
                return last

            def newton(chain, v, r, t):
                chain(nc.vector.tensor_tensor(t, r, r, ALU.mult))
                chain(nc.vector.tensor_tensor(t, t, v, ALU.mult))
                chain(nc.vector.tensor_scalar(t, t, -0.5, 1.5, ALU.mult, ALU.add))
                chain(nc.vector.tensor_tensor(r, r, t, ALU.mult))

            def gn_aggregate(chain, b, last):
                chain(last)
                nc.vector.memset(gtmp[:, :], 0.0)
                for c in range(CT):
                    done = nc.vector.bn_aggr(mv[:, c, :], st[:, c, :, :].rearrange("p a s -> p (a s)"))
                done.then_inc(stats_ready, 1)

            def gn_mean(chain, u, b):
                src = full(u, "gmean")
                nc.vector.tensor_copy(gmean[:, :], src[:, 0:CT]).then_inc(gmean_ready, 1)
                dve.wait_ge(gmean_ready, b + 1)
                chain(nc.vector.tensor_tensor(gtmp[:, :], mv[:, :, 0], gmean[:, :], ALU.subtract))
                chain(nc.vector.tensor_tensor(gtmp[:, :], gtmp[:, :], gtmp[:, :], ALU.mult))
                nc.vector.tensor_tensor(gve[:, :], gtmp[:, :], mv[:, :, 1], ALU.add).then_inc(stats_ready, 1)

            def gn_var(chain, u, b):
                src = full(u, "gvar")
                nc.vector.tensor_scalar(gvar[:, :], src[:, 0:CT], EPS, None, ALU.add).then_inc(gvar_ready, 1)
                dve.wait_ge(sqrt_done, b + 1)
                chain(nc.vector.reciprocal(rstd[:, :], gsq[:, :]))
                newton(chain, gvar[:, :], rstd[:, :], gtmp[:, :])
                for c in range(CT):
                    last = nc.vector.tensor_scalar(w1e[:, c, :], w1T[:, c, :], rstd[:, c:c + 1], None, ALU.mult)
                last.then_inc(w1e_ready, 1)
                chain(nc.vector.tensor_tensor(gtmp[:, :], gmean[:, :], rstd[:, :], ALU.mult))
                chain(nc.vector.tensor_tensor(bnew[:, :], pbi[:, 4:8], gtmp[:, :], ALU.subtract))

            def gn_bias(u, b):
                src = full(u, "bias1")
                nc.vector.tensor_tensor(nb1[:, :], pbi[:, 0:1], src[:, 0:1], ALU.subtract).then_inc(nb1_ready, 1)

            def keep_for_output(chain):
                chain(nc.vector.tensor_copy(rcur[:, :], rstd[:, :]))
                chain(nc.vector.tensor_scalar(r1cur[:, :], rstd[:, :], 1.0, None, ALU.add))
                chain(nc.vector.tensor_copy(bcur[:, :], bnew[:, :]))

            def front(chain, u, b, with_h2):
                for name in FRONT:
                    kind, j = name[0], int(name[1])
                    if kind == "q":
                        src = full(u, name)
                        dve.wait_ge(qh_ready, b * NCH + j + 1)
                        if j >= 2:
                            dve.wait_ge(qparts_ready, b * NCH + j - 1)
                        nc.vector.scalar_tensor_tensor(r1[:, j % 2, :], src[0:QC, :], pbi[0:QC, 2:3],
                                                       q0[:, j * CHUNK:(j + 1) * CHUNK],
                                                       ALU.add, ALU.subtract).then_inc(r1_ready, 1)
                    elif kind == "k":
                        src = full(u, name)
                        if j == 0 and with_h2:
                            dve.wait_ge(h_stored[1], b * (8 * NQ))
                        n = CHUNK // P
                        kv = src[:, 0:n * KV].rearrange("p (n c) -> p n c", c=KV)
                        chain(nc.vector.tensor_copy(kS[:, j * n:(j + 1) * n, :], kv[:, :, DV:KV]))
                        nc.vector.tensor_tensor(vS[:, j * n:(j + 1) * n, :], kv[:, :, 0:DV],
                                                vbias[:, :].unsqueeze(1).to_broadcast([P, n, DV]),
                                                ALU.add).then_inc(vs_ready, 1)
                        softmax_max(chain, j)
                        if j:
                            softmax_sum(chain, b, j - 1)

            def k_chunk(j):
                n = CHUNK // P
                k, m = kS[:, j * n:(j + 1) * n, :], kst[:, j * n:(j + 1) * n]
                return k, m, m.unsqueeze(2).to_broadcast([P, n, DK])

            def softmax_max(chain, j):
                k, m, spread = k_chunk(j)
                chain(nc.vector.reduce_max(m, k, AX_X))
                nc.vector.tensor_tensor(k, k, spread, ALU.subtract).then_inc(kmax_done, 1)

            def softmax_sum(chain, b, j):
                k, m, spread = k_chunk(j)
                dve.wait_ge(kexp_done, b * NCH + j + 1)
                chain(nc.vector.reduce_sum(m, k, AX_X))
                chain(nc.vector.reciprocal(m, m))
                nc.vector.tensor_tensor(k, k, spread, ALU.mult).then_inc(soft_ready, 1)

            def lam(chain, u, b, with_stats):
                def move(i):
                    full(u, f"w{i}.{VECTOR_PART}")
                    move_weights(nc.vector.tensor_copy, u, i, VECTOR_PART).then_inc(w_by_dve, 1)

                dve.wait_ge(pool_out, b * NPOOL + HEAD)
                for i in range(UNITS):
                    if i < UNITS - 1:
                        move(i + 1)
                    q, t = divmod(i, NT)
                    if t == NT - 1:
                        dve.wait_ge(half_done, b * (2 * UNITS) + 2 * i + 2)
                        if q >= 2:
                            dve.wait_ge(h_stored[q % 2], b * (8 * NQ) + 16 * (q // 2))
                        move_sums(nc.vector.tensor_copy, q, 1).then_inc(sums_out[1], 1)
                    if with_stats and i in STAT_STEPS:
                        n = STAT_STEPS.index(i)
                        last = stats_part(b + 1, n)
                        if n == len(STAT_STEPS) - 1:
                            gn_aggregate(chain, b + 1, last)
                    if with_stats:
                        if GN_AFTER.get(i) == "gmean":
                            gn_mean(chain, u, b + 1)
                        if GN_AFTER.get(i) == "gvar":
                            gn_var(chain, u, b + 1)
                        if GN_AFTER.get(i) == "bias1":
                            gn_bias(u, b + 1)

            def output(chain, u, b, softmax):
                for n in range(NCH * CT):
                    j, t = divmod(n, CT)
                    if t == 0:
                        dve.wait_ge(res_in[j], b * 16 + 16)
                    src = full(u, f"o{j}.{t}")
                    if n in POOL_TILES:
                        i = POOL_TILES.index(n)
                        if i >= 2:
                            dve.wait_ge(pool_out, b * NPOOL + HEAD + i - 1)
                        nc.vector.scalar_tensor_tensor(h1[:, i % 2, :], X[:, j, t, :], rcur[:, t:t + 1],
                                                       src[:, :], ALU.mult, ALU.add).then_inc(half_sum, 1)
                    else:
                        i = VEC_TILES.index(n)
                        if i:
                            dve.wait_ge(out_ready, b * NVEC + i)
                        nc.vector.scalar_tensor_tensor(T[:, :], X[:, j, t, :], r1cur[:, t:t + 1], src[:, :],
                                                       ALU.mult, ALU.add).then_inc(whole_sum, 1)
                        dve.wait_ge(whole_sum, b * NVEC + HEAD + i + 1)
                        nc.vector.scalar_tensor_tensor(X[:, j, t, :], T[:, :], bcur[:, t:t + 1], X[:, j, t, :],
                                                       ALU.add, ALU.max).then_inc(out_ready, 1)
                    if softmax and n == SUM_AFTER:
                        softmax_sum(chain, b + 1, NCH - 1)
                dve.wait_ge(out_ready, b * NVEC + NVEC)
                dve.wait_ge(half_relu, b * NPOOL + NPOOL)

            dve.sem_inc(whole_sum, HEAD)
            dve.sem_inc(half_sum, HEAD)
            dve.sem_inc(sums_out[1], HEAD)
            chain = Chain(0)
            nc.vector.memset(vX[:, :, :, :], 0.0).then_inc(setup_zero, 1)
            chain(nc.vector.memset(Epad[:, :], 0.0))
            chain(nc.vector.memset(Elast[:, :, :], 0.0))
            dve.wait_ge(setup_in, N_SETUP_IN)
            g, be, m, v = (par[:, a, :] for a in range(4))
            nc.vector.tensor_scalar(v, v, EPS, None, ALU.add).then_inc(setup_dve, 1)
            dve.wait_ge(setup_act, 1)
            chain(nc.vector.reciprocal(g8[:, 0, :], psc[:, :]))
            newton(chain, v, g8[:, 0, :], g8[:, 1, :])
            chain(nc.vector.tensor_tensor(psc[:, :], g8[:, 0, :], g, ALU.mult))
            chain(nc.vector.tensor_tensor(g8[:, 2, :], m, psc[:, :], ALU.mult))
            chain(nc.vector.tensor_tensor(pbi[:, :], be, g8[:, 2, :], ALU.subtract))
            chain(nc.vector.tensor_scalar(w1r, w1r, psc[:, 0:1], None, ALU.mult))
            for t in range(CT):
                nc.vector.tensor_scalar(w3r[:, t, :], w3r[:, t, :], psc[:, 4 + t:5 + t], None, ALU.mult)
            nc.vector.tensor_scalar(wqr, wqr, psc[0:QC, 2:3], None, ALU.mult)
            chain(nc.vector.tensor_scalar(wkvr[0:DV, :], wkvr[0:DV, :], psc[0:DV, 3:4], None, ALU.mult))
            nc.vector.tensor_copy(vbb, pbi[0:DV, 3:4].to_broadcast([DV, P])).then_inc(setup_scaled, 1)
            chain(nc.vector.tensor_copy(epart[0], emb6))
            chain(nc.vector.tensor_tensor(eres, emb6, epart[0], ALU.subtract))
            nc.vector.tensor_copy(epart[1], eres).then_inc(setup_parts, 1)
            dve.wait_ge(setup_parts, 1)
            nc.vector.tensor_tensor(epart[2], eres, epart[1], ALU.subtract).then_inc(setup_parts, 2)
            dve.wait_ge(setup_pe, 1)
            nc.vector.tensor_copy(w1T[:, :, :].rearrange("p c n -> p (c n)"), ring[0][:, 0:HALF])
            nc.vector.tensor_copy(w3T[:, :, :].rearrange("p c n -> p (c n)"), ring[0][:, HALF:2 * HALF])
            nc.vector.tensor_copy(wqT[:, :], ring[1][:, 0:QC])
            nc.vector.tensor_copy(wkvT[:, :], ring[1][:, QC:QC + KV])
            chain(nc.vector.tensor_copy(vbias[:, :], ring[1][:, P:P + DV]))
            dve.wait_ge(setup_edma, 16 * len(SPLIT))
            chain(nc.vector.tensor_copy(Epad[:, EOFF:EOFF + R * WY].rearrange("p (b a) -> p b a", a=WY)[:, :, 0:R],
                                        Esel.rearrange("p (a b) -> p b a", a=R)))
            dve.wait_ge(setup_pool, 4)
            for yo in range(BY):
                for xo in range(BX):
                    e0 = EOFF + (NT - 1) * P - xo * WY - yo
                    nc.vector.tensor_copy(Elast[:, yo * BX + xo, DK:KC], Epad[:, e0:e0 + LASTW])
            chain(nc.vector.tensor_copy(Elast[:, :, 0:DK], dlt.unsqueeze(1).to_broadcast([NE, PIX, DK])))
            u = uses_before_loop()
            for n in range(8):
                last = stats_part(0, n)
            gn_aggregate(chain, 0, last)
            gn_mean(chain, u, 0)
            gn_var(chain, u, 0)
            gn_bias(u, 0)
            keep_for_output(chain)
            front(chain, u, 0, False)
            softmax_sum(chain, 0, NCH - 1)
            pre = chain.n
            LOOP_LINKS = 29
            with dve.Fori(0, B - 1) as b:
                chain = Chain(b * LOOP_LINKS + pre)
                u = uses_in_loop(b)
                lam(chain, u, b, True)
                front(chain, u, b + 1, True)
                output(chain, u, b, True)
                keep_for_output(chain)
                assert chain.n == LOOP_LINKS, chain.n
            chain = Chain((B - 1) * LOOP_LINKS + pre)
            u = uses_after_loop()
            lam(chain, u, B - 1, False)
            output(chain, u, B - 1, False)

        @block.gpsimd
        def _(pool):
            nc.gpsimd.memset(par[:, :, :], 1.0).then_inc(setup_pool, 1)
            nc.gpsimd.memset(ident[:, :], 0.0).then_inc(setup_pool, 1)
            pool.wait_ge(setup_pool, 2)
            nc.gpsimd.affine_select(out=ident[:, :], in_=ident[:, :], compare_op=ALU.not_equal, fill=1.0, base=0,
                                    pattern=[[-1, P]], channel_multiplier=1).then_inc(setup_pool, 1)
            nc.gpsimd.memset(dlt, 0.0).then_inc(setup_gp, 1)
            n = 1
            for g in range(NPART):
                pool.wait_ge(setup_gp, n)
                nc.gpsimd.affine_select(out=dlt, in_=dlt, compare_op=ALU.not_equal, fill=1.0, base=-g * DK,
                                        pattern=[[-1, DK]], channel_multiplier=1).then_inc(setup_gp, 1)
                n += 1
            nc.gpsimd.memset(grp[:, :], 1.0 / CPG).then_inc(setup_gp, 1)
            nc.gpsimd.memset(zeros[:, :], 0.0).then_inc(setup_gp, 1)
            n += 2
            gv = grp[:, :].rearrange("p (a c) -> p a c", c=CPG)
            pool.wait_ge(setup_gp, n)
            nc.gpsimd.affine_select(out=gv, in_=gv, compare_op=ALU.is_ge, fill=0.0, base=0,
                                    pattern=[[-CPG, P // CPG], [0, CPG]], channel_multiplier=1).then_inc(setup_gp, 1)
            n += 1
            pool.wait_ge(setup_gp, n)
            nc.gpsimd.affine_select(out=gv, in_=gv, compare_op=ALU.is_ge, fill=0.0, base=CPG - 1,
                                    pattern=[[CPG, P // CPG], [0, CPG]], channel_multiplier=-1).then_inc(setup_pool, 1)

            def split_q(b, outputs, after_content):
                pool.wait_ge(pool_out, outputs * NPOOL + HEAD)
                if after_content:
                    pool.wait_ge(content_ready, b)
                for j in range(NCH):
                    cols = slice(j * CHUNK, (j + 1) * CHUNK)
                    pool.wait_ge(qm_done, b * NCH + j + 1)
                    nc.gpsimd.tensor_tensor(q12[:, 1, cols], r1[:, j % 2, :], q12[:, 0, cols], ALU.subtract)\
                        .then_inc(qparts_ready, 1)

            def output(b, splits):
                pool.wait_ge(qparts_ready, splits * NCH)
                for i, n in enumerate(POOL_TILES):
                    j, t = divmod(n, CT)
                    pool.wait_ge(half_relu, b * NPOOL + i + 1)
                    nc.gpsimd.tensor_tensor(X[:, j, t, :], X[:, j, t, :], h1[:, i % 2, :], ALU.add)\
                        .then_inc(pool_out, 1)

            def content(b):
                pool.wait_ge(cl_ready, b + 1)
                spread, none = (a[:, :].unsqueeze(1).to_broadcast([DK, NXB * NBY, DV]) for a in (clS, zeros))
                nc.gpsimd.tensor_tensor(V[0:DK, NT - 1, :, :].rearrange("k xb (yb v) -> k (xb yb) v", v=DV),
                                        spread, none, ALU.add).then_inc(content_ready, 1)

            pool.sem_inc(pool_out, HEAD)
            split_q(0, 0, False)
            pool.wait_ge(qparts_ready, NCH)
            content(0)
            with pool.Fori(0, B - 1) as b:
                split_q(b + 1, b, True)
                output(b, b + 2)
                pool.wait_ge(pool_out, b * NPOOL + NPOOL + HEAD)
                content(b + 1)
            output(B - 1, B)


_IN = ["x"] + ["L0_conv_" + n for n in (
    "conv1_w bn1_g bn1_b bn1_m bn1_v q_w bnq_g bnq_b bnq_m bnq_v k_w v_w bnv_g bnv_b bnv_m bnv_v emb "
    "bn2_g bn2_b bn2_m bn2_v conv3_w bn3_g bn3_b bn3_m bn3_v").split()]


def kernel(**inputs):
    import numpy as np
    import concourse.bacc as bacc
    from concourse.bass_utils import run_bass_kernel_spmd

    nc = bacc.Bacc("TRN2", target_bir_lowering=False, num_devices=1, dynamic_dma_scratch_size=1024)
    arrays, ap = {}, {}
    for name in _IN:
        a = np.ascontiguousarray(inputs[name])
        arrays[name + "_dram"] = a
        ap[name.replace("L0_conv_", "")] = nc.dram_tensor(name + "_dram", a.shape, mybir.dt.from_np(a.dtype),
                                                          kind="ExternalInput").ap()
    out = nc.dram_tensor("out_dram", inputs["x"].shape, F32, kind="ExternalOutput").ap()
    bn = {n: [ap[f"bn{n}_{a}"] for a in "gbmv"] for n in ("1", "2", "3", "q", "v")}
    lambda_block(nc, ap["x"], ap["conv1_w"], bn["1"], ap["q_w"], bn["q"], ap["k_w"], ap["v_w"], bn["v"],
                 ap["emb"], bn["2"], ap["conv3_w"], bn["3"], out)
    got = run_bass_kernel_spmd(nc, [arrays], core_ids=[0])
    return got.results[0]["out_dram"]
```
